# Optimizing a Trainium2 kernel written in Bass

```python
import numpy as np
import jax
import jax.numpy as jnp

def _softmax(x, axis=-1):
    return jax.nn.softmax(x, axis=axis)

def _gelu(x):
    return jax.nn.gelu(x, approximate=True)

def _silu(x):
    return jax.nn.silu(x)

def _sigmoid(x):
    return jax.nn.sigmoid(x)

def _layernorm(x, axis=-1, eps=1e-05):
    m = jnp.mean(x, axis=axis, keepdims=True)
    v = jnp.var(x, axis=axis, keepdims=True)
    return (x - m) / jnp.sqrt(v + eps)

def _scatter_add(tgt, idx, src, axis=0):
    return tgt.at[idx].add(src)

def _segment_sum(src, seg, n):
    return jax.ops.segment_sum(src, seg, n)
kernel_name = 'mk_flamingo_gated_d2_seqx_r4_26f819'

def setup_inputs(seed: int=0):
    np.random.seed(seed)
    _w = jnp.asarray

    def _rec_inputs():
        import jax
        import jax.numpy as jnp
        _rk = jax.random.key(seed)
        x = 7.22e-05 + 1 * jax.random.normal(jax.random.fold_in(_rk, 1), (16, 256, 256), jnp.float32)
        _lenS = 256 - jax.random.randint(jax.random.fold_in(_rk, 7), (16,), 0, max(1, 256 // 4) + 1, jnp.int32)
        _lenS2 = 256 - jax.random.randint(jax.random.fold_in(_rk, 8), (16,), 0, max(1, 256 // 4) + 1, jnp.int32)
        _ctx_1024P = jax.random.normal(jax.random.fold_in(_rk, 11), (16, 16, 256), jnp.float32)
        _ctx_1024c = jax.random.dirichlet(jax.random.fold_in(_rk, 511), 0.3 * jnp.ones((16,), jnp.float32), (16, 256))
        _ctx_1024t = jnp.einsum('bsk,bkd->bsd', _ctx_1024c, _ctx_1024P)
        _ctx_1024t = _ctx_1024t * jax.lax.rsqrt(jnp.mean(jnp.square(_ctx_1024t)) + 1e-12) * 0.953939
        ctx_1024 = 4.13588e-05 + 0.999923 * (_ctx_1024t + 0.3 * jax.random.normal(jax.random.fold_in(_rk, 611), (16, 256, 256), jnp.float32))
        _validS = jnp.arange(256)[None, :] < _lenS[:, None]
        _validS2 = jnp.arange(256)[None, :] < _lenS2[:, None]
        _causal = jnp.tril(jnp.ones((256, 256), dtype=bool))
        mask_SxS2_ff0 = jnp.where(jnp.ones((256, 256), dtype=bool), 0.0, -1000000000.0).astype(jnp.float32)
        mask_BxS2_bf0 = jnp.logical_not(jnp.ones((16, 256), dtype=bool))
        _g = jax.random.normal(jax.random.fold_in(_rk, 9001), (2, 2), jnp.float32)
        _g = jnp.sign(_g) * jnp.maximum(jnp.abs(_g), 1.0) + (_g == 0) * 1.0
        g_xattn = _g[0]
        g_ffn = _g[1]
        return (x, ctx_1024, mask_SxS2_ff0, mask_BxS2_bf0, g_xattn, g_ffn)
    x, ctx_1024, mask_SxS2_ff0, mask_BxS2_bf0, g_xattn, g_ffn = _rec_inputs()

    def _L0_xattn_setup():
        import jax, jax.numpy as jnp
        import numpy as np
        D_MODEL = 256
        NUM_HEADS = 16
        HEAD_DIM = D_MODEL // NUM_HEADS
        B, TQ, TK = (4, 512, 512)
        key = jax.random.key(seed)
        ks = jax.random.split(key, 6)
        s = 1.0 / np.sqrt(D_MODEL)
        return {'x_q': jax.random.normal(ks[0], (B, TQ, D_MODEL), dtype=jnp.float32), 'x_kv': jax.random.normal(ks[1], (B, TK, D_MODEL), dtype=jnp.float32), 'attn_mask': jnp.zeros((TQ, TK), dtype=jnp.float32), 'key_padding_mask': jnp.zeros((B, TK), dtype=bool), 'Wq': jax.random.normal(ks[2], (D_MODEL, D_MODEL), dtype=jnp.float32) * s, 'Wk': jax.random.normal(ks[3], (D_MODEL, D_MODEL), dtype=jnp.float32) * s, 'Wv': jax.random.normal(ks[4], (D_MODEL, D_MODEL), dtype=jnp.float32) * s, 'Wo': jax.random.normal(ks[5], (D_MODEL, D_MODEL), dtype=jnp.float32) * s}
    _L0_xattn_all = _L0_xattn_setup()
    _L0_xattn_in = {k: v for k, v in _L0_xattn_all.items() if k in ('Wq', 'Wk', 'Wv', 'Wo')}
    del _L0_xattn_all

    def _L0_ffn_setup():
        import jax, jax.numpy as jnp
        import numpy as np
        TOP_K = 2
        key = jax.random.key(seed)
        ks = jax.random.split(key, 5)
        B, S, D, I, E = (4, 128, 256, 1024, 8)
        x = jax.random.normal(ks[0], (B, S, D), dtype=jnp.float32)
        gate_w = jax.random.normal(ks[1], (E, D), dtype=jnp.float32) * 0.02
        w1 = jax.random.normal(ks[2], (E, I, D), dtype=jnp.float32) * 0.02
        w2 = jax.random.normal(ks[3], (E, D, I), dtype=jnp.float32) * 0.02
        w3 = jax.random.normal(ks[4], (E, I, D), dtype=jnp.float32) * 0.02
        return {'x': x, 'gate_w': gate_w, 'w1': w1, 'w2': w2, 'w3': w3}
    _L0_ffn_all = _L0_ffn_setup()
    _L0_ffn_in = {k: v for k, v in _L0_ffn_all.items() if k in ('gate_w', 'w1', 'w2', 'w3')}
    del _L0_ffn_all

    def _L1_xattn_setup():
        import jax, jax.numpy as jnp
        import numpy as np
        D_MODEL = 256
        N_HEADS = 16
        D_K = D_MODEL // N_HEADS
        key = jax.random.key(seed)
        ks = jax.random.split(key, 11)
        B, S = (2, 512)
        scale = 1.0 / np.sqrt(D_MODEL)
        return {'query': jax.random.normal(ks[0], (B, S, D_MODEL), jnp.float32), 'key': jax.random.normal(ks[1], (B, S, D_MODEL), jnp.float32), 'value': jax.random.normal(ks[2], (B, S, D_MODEL), jnp.float32), 'w_q': jax.random.normal(ks[3], (D_MODEL, D_MODEL), jnp.float32) * scale, 'b_q': jnp.zeros((D_MODEL,), jnp.float32), 'w_k': jax.random.normal(ks[4], (D_MODEL, D_MODEL), jnp.float32) * scale, 'b_k': jnp.zeros((D_MODEL,), jnp.float32), 'w_v': jax.random.normal(ks[5], (D_MODEL, D_MODEL), jnp.float32) * scale, 'b_v': jnp.zeros((D_MODEL,), jnp.float32), 'w_o': jax.random.normal(ks[6], (D_MODEL, D_MODEL), jnp.float32) * scale, 'b_o': jnp.zeros((D_MODEL,), jnp.float32)}
    _L1_xattn_all = _L1_xattn_setup()
    _L1_xattn_in = {k: v for k, v in _L1_xattn_all.items() if k in ('w_q', 'b_q', 'w_k', 'b_k', 'w_v', 'b_v', 'w_o', 'b_o')}
    del _L1_xattn_all

    def _L1_ffn_setup():
        import jax, jax.numpy as jnp
        import numpy as np
        HIDDEN = 256
        INNER = 1024

        def _weight_quant(w):
            scale = 1.0 / jnp.clip(jnp.mean(jnp.abs(w)), 1e-05)
            wq = jnp.clip(jnp.round(w * scale), -1.0, 1.0) / scale
            return w + jax.lax.stop_gradient(wq - w)

        def _act_quant(x):
            scale = 127.0 / jnp.clip(jnp.max(jnp.abs(x), axis=-1, keepdims=True), 1e-05)
            xq = jnp.clip(jnp.round(x * scale), -128.0, 127.0) / scale
            return x + jax.lax.stop_gradient(xq - x)

        def _bitlinear(x, w):
            return jnp.einsum('bsi,oi->bso', _act_quant(x), _weight_quant(w))
        key = jax.random.key(seed)
        k0, k1, k2, k3 = jax.random.split(key, 4)
        x = jax.random.normal(k0, (4, 512, HIDDEN), dtype=jnp.float32)
        w_gate = jax.random.normal(k1, (INNER, HIDDEN), dtype=jnp.float32) / np.sqrt(HIDDEN)
        w_up = jax.random.normal(k2, (INNER, HIDDEN), dtype=jnp.float32) / np.sqrt(HIDDEN)
        w_down = jax.random.normal(k3, (HIDDEN, INNER), dtype=jnp.float32) / np.sqrt(INNER)
        return {'x': x, 'w_gate': w_gate, 'w_up': w_up, 'w_down': w_down}
    _L1_ffn_all = _L1_ffn_setup()
    _L1_ffn_in = {k: v for k, v in _L1_ffn_all.items() if k in ('w_gate', 'w_up', 'w_down')}
    del _L1_ffn_all
    return {'x': x, 'ctx_1024': ctx_1024, 'mask_SxS2_ff0': mask_SxS2_ff0, 'mask_BxS2_bf0': mask_BxS2_bf0, 'g_xattn': g_xattn, 'g_ffn': g_ffn, 'L0_xattn_Wq': _L0_xattn_in['Wq'], 'L0_xattn_Wk': _L0_xattn_in['Wk'], 'L0_xattn_Wv': _L0_xattn_in['Wv'], 'L0_xattn_Wo': _L0_xattn_in['Wo'], 'L0_ffn_gate_w': _L0_ffn_in['gate_w'], 'L0_ffn_w1': _L0_ffn_in['w1'], 'L0_ffn_w2': _L0_ffn_in['w2'], 'L0_ffn_w3': _L0_ffn_in['w3'], 'L1_xattn_w_q': _L1_xattn_in['w_q'], 'L1_xattn_b_q': _L1_xattn_in['b_q'], 'L1_xattn_w_k': _L1_xattn_in['w_k'], 'L1_xattn_b_k': _L1_xattn_in['b_k'], 'L1_xattn_w_v': _L1_xattn_in['w_v'], 'L1_xattn_b_v': _L1_xattn_in['b_v'], 'L1_xattn_w_o': _L1_xattn_in['w_o'], 'L1_xattn_b_o': _L1_xattn_in['b_o'], 'L1_ffn_w_gate': _L1_ffn_in['w_gate'], 'L1_ffn_w_up': _L1_ffn_in['w_up'], 'L1_ffn_w_down': _L1_ffn_in['w_down']}

def reference(x, ctx_1024, mask_SxS2_ff0, mask_BxS2_bf0, g_xattn, g_ffn, L0_xattn_Wq, L0_xattn_Wk, L0_xattn_Wv, L0_xattn_Wo, L0_ffn_gate_w, L0_ffn_w1, L0_ffn_w2, L0_ffn_w3, L1_xattn_w_q, L1_xattn_b_q, L1_xattn_w_k, L1_xattn_b_k, L1_xattn_w_v, L1_xattn_b_v, L1_xattn_w_o, L1_xattn_b_o, L1_ffn_w_gate, L1_ffn_w_up, L1_ffn_w_down):
    import jax
    import jax.numpy as jnp

    def _L0_xattn_ref(x_q, x_kv, attn_mask, key_padding_mask, Wq, Wk, Wv, Wo):
        import jax, jax.numpy as jnp
        import numpy as np
        D_MODEL = 256
        NUM_HEADS = 16
        HEAD_DIM = D_MODEL // NUM_HEADS
        B, TQ, TK = (4, 512, 512)
        b, tq, d = x_q.shape
        tk = x_kv.shape[1]
        h, hd = (NUM_HEADS, HEAD_DIM)
        q = (x_q @ Wq.T).reshape(b, tq, h, hd).transpose(0, 2, 1, 3)
        k = (x_kv @ Wk.T).reshape(b, tk, h, hd).transpose(0, 2, 1, 3)
        v = (x_kv @ Wv.T).reshape(b, tk, h, hd).transpose(0, 2, 1, 3)
        scores = jnp.einsum('bhqd,bhkd->bhqk', q, k) / jnp.sqrt(jnp.float32(hd))
        scores = scores + attn_mask
        scores = jnp.where(key_padding_mask[:, None, None, :], -jnp.inf, scores)
        w = jax.nn.softmax(scores, axis=-1)
        out = jnp.einsum('bhqk,bhkd->bhqd', w, v)
        out = out.transpose(0, 2, 1, 3).reshape(b, tq, d)
        return out @ Wo.T

    def _L0_ffn_ref(x, gate_w, w1, w2, w3):
        import jax, jax.numpy as jnp
        import numpy as np
        TOP_K = 2
        bsz, seq, dim = x.shape
        xt = x.reshape(-1, dim)
        scores = jnp.einsum('td,ed->te', xt, gate_w)
        probs = jax.nn.softmax(scores, axis=-1)
        expert_weights, expert_indices = jax.lax.top_k(probs, TOP_K)
        expert_weights = expert_weights / expert_weights.sum(-1, keepdims=True)
        x1 = jax.nn.silu(jnp.einsum('ti,eoi->teo', xt, w1))
        x3 = jnp.einsum('ti,eoi->teo', xt, w3)
        expert_outs = jnp.einsum('teo,eio->tei', x1 * x3, w2)
        sel = jnp.take_along_axis(expert_outs, expert_indices[:, :, None], axis=1)
        out = jnp.einsum('tai,ta->ti', sel, expert_weights)
        return out.reshape(bsz, seq, dim)

    def _L1_xattn_ref(query, key, value, w_q, b_q, w_k, b_k, w_v, b_v, w_o, b_o):
        import jax, jax.numpy as jnp
        import numpy as np
        D_MODEL = 256
        N_HEADS = 16
        D_K = D_MODEL // N_HEADS
        B, S, _ = query.shape

        def proj(x, w, b):
            y = jnp.einsum('bsd,ed->bse', x, w) + b
            return y.reshape(B, -1, N_HEADS, D_K).transpose(0, 2, 1, 3)
        q = proj(query, w_q, b_q)
        k = proj(key, w_k, b_k)
        v = proj(value, w_v, b_v)
        scores = jnp.einsum('bhqd,bhkd->bhqk', q, k) / np.sqrt(D_K)
        attn = jax.nn.softmax(scores, axis=-1)
        out = jnp.einsum('bhqk,bhkd->bhqd', attn, v)
        out = out.transpose(0, 2, 1, 3).reshape(B, S, D_MODEL)
        out = jnp.einsum('bsd,ed->bse', out, w_o) + b_o
        return out

    def _L1_ffn_ref(x, w_gate, w_up, w_down):
        import jax, jax.numpy as jnp
        import numpy as np
        HIDDEN = 256
        INNER = 1024

        def _weight_quant(w):
            scale = 1.0 / jnp.clip(jnp.mean(jnp.abs(w)), 1e-05)
            wq = jnp.clip(jnp.round(w * scale), -1.0, 1.0) / scale
            return w + jax.lax.stop_gradient(wq - w)

        def _act_quant(x):
            scale = 127.0 / jnp.clip(jnp.max(jnp.abs(x), axis=-1, keepdims=True), 1e-05)
            xq = jnp.clip(jnp.round(x * scale), -128.0, 127.0) / scale
            return x + jax.lax.stop_gradient(xq - x)

        def _bitlinear(x, w):
            return jnp.einsum('bsi,oi->bso', _act_quant(x), _weight_quant(w))
        gate = jax.nn.silu(_bitlinear(x, w_gate))
        up = _bitlinear(x, w_up)
        return _bitlinear(gate * up, w_down)
    x = x + jnp.tanh(g_xattn[0]) * _L0_xattn_ref(_layernorm(x, axis=-1), ctx_1024, mask_SxS2_ff0, mask_BxS2_bf0, L0_xattn_Wq, L0_xattn_Wk, L0_xattn_Wv, L0_xattn_Wo)
    x = x + jnp.tanh(g_ffn[0]) * _L0_ffn_ref(_layernorm(x, axis=-1), L0_ffn_gate_w, L0_ffn_w1, L0_ffn_w2, L0_ffn_w3)
    x = x + jnp.tanh(g_xattn[1]) * _L1_xattn_ref(_layernorm(x, axis=-1), ctx_1024, ctx_1024, L1_xattn_w_q, L1_xattn_b_q, L1_xattn_w_k, L1_xattn_b_k, L1_xattn_w_v, L1_xattn_b_v, L1_xattn_w_o, L1_xattn_b_o)
    x = x + jnp.tanh(g_ffn[1]) * _L1_ffn_ref(_layernorm(x, axis=-1), L1_ffn_w_gate, L1_ffn_w_up, L1_ffn_w_down)
    return x

_drawn_inputs = setup_inputs


def setup_inputs(seed=0):
    import zlib

    import numpy as np

    out = dict(_drawn_inputs(seed))
    spreads = {'mask_SxS2_ff0': (0.0, 0.8),
     'g_ffn': (-1.0, 0.6),
     'L1_xattn_b_q': (0.0, 0.437),
     'L1_xattn_b_k': (0.0, 0.8),
     'L1_xattn_b_v': (0.0, 0.1),
     'L1_xattn_b_o': (0.0, 0.1)}
    factors = {'L0_ffn_gate_w': 4.083, 'L0_ffn_w1': 3.625, 'L0_ffn_w2': 3.589, 'L0_ffn_w3': 3.589}
    for name, (base, spread) in spreads.items():
        noise = np.random.default_rng([zlib.crc32(name.encode()), seed]).standard_normal(out[name].shape)
        drawn = base * np.exp(spread * noise) if base else spread * noise
        out[name] = jnp.asarray(drawn.astype(out[name].dtype))
    for name, factor in factors.items():
        out[name] = (out[name] * factor).astype(out[name].dtype)
    return out
```

```python
from contextlib import ExitStack

import numpy as np

import concourse.bass as bass
from concourse import mybir

F32, F16, BF16 = mybir.dt.float32, mybir.dt.float16, mybir.dt.bfloat16
I32, U32, U8 = mybir.dt.int32, mybir.dt.uint32, mybir.dt.uint8
ACT = mybir.ActivationFunctionType
ALU = mybir.AluOpType
X = mybir.AxisListType.X

P = 128
B, S, D = 16, 256, 256
TOK = B * S
H, HD = 16, 16
PAIRS = H // 2
C2 = D // P
E, INNER = 8, 1024
NI = INNER // P
WSC = 64.0
LOGIT = 1.0 / (WSC * WSC * 4.0)
SHIFT = 256.0
MASKED = -30000.0
TILE = 256
REGION = TOK + TILE
NT = (2 * TOK + E * (TILE - 1)) // TILE
NTP = 40
DATA, KPM, SHA = 96, 96, 97
STACK = 99
RND = 12582912.0
EPS = 1e-5


class Misc:
    SECOND = ("M1", "K", "UT0", "UT1", "OT", "WO", "RK")

    def __init__(self, layer, base):
        self.steps = {0: "M1", 2: "K", 4: "UT0", 5: "XT", 6: "UT1", 7: "Q", 8: "OT", 9: "V", 10: "WO", 11: "M0"}
        if layer == 0:
            self.steps |= {1: "GT", 3: "GS", 12: "RK"}
        self.lag = {"M1": 1, "XT": -1, "UT0": 2, "Q": -1, "UT1": 2, "K": -1, "OT": 2, "V": -1, "M0": 0, "WO": 2,
                    "RK": 3, "GT": 3, "GS": 3}
        self.order = [self.steps[s] for s in sorted(self.steps)]
        self.start, n = {}, base
        for i in range(-1, B + 4):
            self.start[i] = n
            n += sum(self.has(i, name) for name in self.order)
        self.end = n
        self.first_full = 4
        self.last_full = B - 4

    def has(self, i, name):
        return 0 <= i - self.lag[name] < B

    def before(self, i, name):
        at = self.order.index(name)
        if isinstance(i, int):
            return self.start[i] + sum(self.has(i, x) for x in self.order[:at])
        return i * len(self.order) + (self.start[self.first_full] - self.first_full * len(self.order) + at)

    def previous(self, i, name):
        at = self.order.index(name)
        back = [(i, x) for x in reversed(self.order[:at])] + [(i - 1, x) for x in reversed(self.order)]
        back = [(k, x) for k, x in back if (x in self.SECOND) == (name in self.SECOND)]
        if not isinstance(i, int):
            return back[0]
        return next(((k, x) for k, x in back if self.has(k, x)), None)


def build(nc, a, out):
    ctx = ExitStack()
    with ctx:
        def sb(name, shape, dt):
            return ctx.enter_context(nc.sbuf_tensor(name, shape, dt))

        def pb(name, shape, dt):
            return ctx.enter_context(nc.psum_tensor(name, shape, dt))

        def sem(name):
            return ctx.enter_context(nc.semaphore(name))

        def dram(name, shape, dt):
            return nc.dram_tensor(name, shape, dt).ap()

        x1_d = dram("x1_d", [TOK, D], F32)
        x2_d = dram("x2_d", [TOK, D], F32)
        x3_d = dram("x3_d", [TOK, D], F32)
        routed_d = dram("routed_d", [E * REGION, 2 * D], F16)
        y_d = dram("y_d", [NT * TILE, D], F32)
        ws_d = dram("ws_d", [3 * E, P, 4096], F16)
        kpm_d = dram("kpm_d", [2 * B, S], F16)

        psS = pb("psS", [P, 2, 512], F32)
        psT = pb("psT", [P, 2, 2, 512], F32)
        psU = pb("psU", [P, 512], F32)
        psM = pb("psM", [P, 512], F32)
        psM16 = psM[:, :].bitcast(F16)
        psH = psT[:, :, :, :].rearrange("p a b n -> p (a b) n")
        psN = psH[:, 3]

        id32 = sb("id32", [P, P], F32)
        id16 = sb("id16", [P, P], F16)
        idb = sb("idb", [P, P], BF16)
        idmask = sb("idmask", [P, P], F16)
        lower = sb("lower", [P, P], F16)
        ones16 = sb("ones16", [P, P], F16)
        aw = sb("aw", [P, 2, 2, 4, C2, D], F16)
        bqk = sb("bqk", [P, 2, C2], F32)
        bv = sb("bv", [P, D], F32)
        bo = sb("bo", [P, D], F32)
        zero = sb("zero", [P, D], F32)
        zero16 = sb("zero16", [P, 2, 2 * D], F16)
        gts = sb("gts", [P, 4], F32)
        tg = sb("tg", [P, 4], F32)
        tg64 = sb("tg64", [P, 4], F32)
        gate = sb("gate", [P, C2, E], F32)
        gatehl = sb("gatehl", [P, 2, C2, E], F16)
        maskf = sb("maskf", [P, C2, S], F32)
        maskh = sb("maskh", [P, C2, S], F16)
        maskT = sb("maskT", [P, C2, S], F32)
        maxmask = sb("maxmask", [P, C2], F32)
        kpm8 = sb("kpm8", [B, S], U8)
        kpmh = sb("kpmh", [B, S], F16)
        kconst = sb("kconst", [2, 2, PAIRS * S], F16)
        qs = sb("qs", [P, 3, PAIRS, S], F16)
        ks = sb("ks", [P, 3, 2, PAIRS, S], F16)
        vv = sb("vv", [P, 3, C2, H, 32], F32)
        mx = sb("mx", [P, 2, C2, 8], F32)
        mt = sb("mt", [8, 2, S], F16)
        lnst = sb("lnst", [P, C2, 6], F32)
        lnmv = sb("lnmv", [P, C2, 2], F32)
        lnrs = sb("lnrs", [P, 2, C2], F32)
        l2st = sb("l2st", [P, C2, 6], F32)
        l2mv = sb("l2mv", [P, C2, 2], F32)
        l2rs = sb("l2rs", [P, 2, C2], F32)
        mhalf = sb("mhalf", [P, C2], F32)
        rden = sb("rden", [P, C2, H], F32)
        w8 = sb("w8", [P, E], F32)
        sc = sb("sc", [P, 2, C2, E], F32)
        eqm = sb("eqm", [P, C2, E], F32)
        top = sb("top", [P, 2, C2], F32)
        wmax = sb("wmax", [P, C2], F32)
        oh = sb("oh", [P, 2, C2, E], F32)
        chosen = sb("chosen", [P, C2, E], F16)
        runb = sb("runb", [P, E], F32)
        rank = sb("rank", [P, C2, E], F32)
        prod = sb("prod", [P, 2, C2, E], F32)
        row = sb("row", [P, 2, C2], F32)
        rowi = sb("rowi", [P, 2, C2], U32)
        OH = sb("OH", [P, B, 2 * C2 * E], F32)
        ROW = sb("ROW", [P, B, 2 * C2], F32)
        TOP = sb("TOP", [P, B, 2 * C2], F32)
        WAB = sb("WAB", [P, 2, B * C2], F32)
        POS = sb("POS", [P, B, 2 * C2], U32)
        gidx = sb("gidx", [P, 4], U32)
        cnt = sb("cnt", [P, E], F32)
        ntile = sb("ntile", [P, E], F32)
        cum = sb("cum", [P, E + 1], F32)
        base = sb("base", [P, E], F32)
        delta = sb("delta", [P, E], F32)
        dbase = sb("dbase", [P, E - 1], F32)
        lim = sb("lim", [P, 1], F32)
        tt = sb("tt", [P, NT], F32)
        ge = sb("ge", [P, NT], F32)
        eid = sb("eid", [P, NT], F32)
        rowf = sb("rowf", [P, NT], F32)
        rowt = sb("rowt", [P, NT], I32)
        eidt = sb("eidt", [P, NT], I32)
        endi = sb("endi", [P, E], I32)
        posf = sb("posf", [P, 4 * B], F32)
        tdif = sb("tdif", [P, B * C2], F32)
        tsum = sb("tsum", [P, B * C2], F32)
        fst = sb("fst", [P, 2048], F32)
        fwt = sb("fwt", [P, 3, 2048], BF16)
        fabs = sb("fabs", [P, 3], F32)
        ones32 = sb("ones32", [P, P], F32)
        fmean = sb("fmean", [P, 3], F32)
        fscale = sb("fscale", [P, 3], F32)
        fdeq = sb("fdeq", [P, 3], F32)
        fst6 = sb("fst6", [P, 6], F32)
        fmv = sb("fmv", [P, 2], F32)
        frs = sb("frs", [P, 2], F32)
        am = sb("am", [P, 4], F32)
        fsc = sb("fsc", [P, 2, 2], F32)
        fd = sb("fd", [P, 2], F32)
        sc2 = sb("sc2", [P, 1], F32)
        rnd = sb("rnd", [P, 1], F32)
        big = sb("big", [P, 2, 3, 2, 2048], F16)
        bigf = big[:, :, :, :, :].rearrange("p a b c n -> p (a b c n)").bitcast(F32)
        pt = bigf[:, 0:4096].rearrange("p (s h n) -> p s h n", s=4, h=2)
        wst = bigf[:, 4096:8192].rearrange("p (s n) -> p s n", s=2)
        wsp = bigf[:, 8192:12288].bitcast(F16).rearrange("p (s l n) -> p s l n", s=2, l=2)
        work = sb("work", [P, 10752], F32)
        at = [0]

        def part(words):
            at[0] += words
            assert at[0] <= 10752
            return work[:, at[0] - words:at[0]]

        xin = part(1536).rearrange("p (s c d) -> p s c d", s=3, c=C2)
        cin = part(1536).rearrange("p (s c d) -> p s c d", s=3, c=C2)
        xn = part(512).rearrange("p (c d) -> p c d", c=C2)
        xhl = part(512).bitcast(F16).rearrange("p (l c n) -> p l c n", l=2, c=C2)
        qhl = part(512).bitcast(F16).rearrange("p (l n) -> p l n", l=2)
        khl = part(512).bitcast(F16).rearrange("p (l n) -> p l n", l=2)
        chl = part(512).bitcast(F16).rearrange("p (l c n) -> p l c n", l=2, c=C2)
        uu = part(1024).rearrange("p (s n) -> p s n", s=2)
        oo = part(512).rearrange("p (c d) -> p c d", c=C2)
        ohl = part(512).bitcast(F16).rearrange("p (l c n) -> p l c n", l=2, c=C2)
        xo = part(512).rearrange("p (c d) -> p c d", c=C2)
        xn1 = part(512).rearrange("p (c d) -> p c d", c=C2)
        xg = part(512).bitcast(F16).rearrange("p (k n) -> p k n", k=4)
        xr_ga = part(1536)
        xr = xr_ga.bitcast(F16).rearrange("p (s c n) -> p s c n", s=3, c=C2)
        ga = xr_ga[:, 0:1024].rearrange("p (k c d) -> p k c d", k=2, c=C2)
        at[0] = 0
        mxr = part(1024).bitcast(F16).rearrange("p (s c n) -> p s c n", s=2, c=C2)
        mxt = part(1024).bitcast(F16).rearrange("p (s k n) -> p s k n", s=2, k=4)
        sg = part(1024).rearrange("p (s n) -> p s n", s=2)
        hb = part(1024).rearrange("p (s n) -> p s n", s=2)
        hhl = part(4096).bitcast(F16).rearrange("p (s l c n) -> p s l c n", s=2, l=2, c=NI)
        ye = part(1024).rearrange("p (s n) -> p s n", s=2)

        s_id = sem("s_id")
        s_const = sem("s_const")
        s_set = sem("s_set")
        s_setw = sem("s_setw")
        s_wh = sem("s_wh")
        s_wl = sem("s_wl")
        s_dset = sem("s_dset")
        s_tg = sem("s_tg")
        s_kpm = sem("s_kpm")
        s_krow = sem("s_krow")
        s_maskt = sem("s_maskt")
        s_ready = sem("s_ready")
        s_apart = sem("s_apart")

        def apart(eng):
            eng.sem_inc(s_apart, 1)

        s_x = [sem(f"s_xin{k}") for k in range(3)]
        s_c = [sem(f"s_cin{k}") for k in range(3)]
        s_ln = sem("s_ln")
        s_var = sem("s_var")
        s_rs = sem("s_rs")
        s_xn = sem("s_xn")
        s_xh = sem("s_xh")
        s_xl = sem("s_xl")
        s_ch = sem("s_ch")
        s_cl = sem("s_cl")
        s_qh = sem("s_qh")
        s_ql = sem("s_ql")
        s_kh = sem("s_kh")
        s_kl = sem("s_kl")
        s_v = sem("s_v")
        s_qst = sem("s_qst")
        s_kst = sem("s_kst")
        s_s = sem("s_s")
        s_mx = sem("s_mx")
        s_mt = sem("s_mt")
        s_sh = sem("s_sh")
        s_t = sem("s_t")
        s_add = sem("s_add")
        s_exp = sem("s_exp")
        s_pv = sem("s_pv")
        s_u = sem("s_u")
        s_rd = sem("s_rd")
        s_o = sem("s_o")
        s_oh = sem("s_oh")
        s_ol = sem("s_ol")
        s_xo = sem("s_xo")
        s_bo = sem("s_bo")
        s_x1 = sem("s_x1")
        s_xst = sem("s_xst")
        s_md = sem("s_md")
        s_l2 = sem("s_l2")
        s_var2 = sem("s_var2")
        s_rs2 = sem("s_rs2")
        s_xn1 = sem("s_xn1")
        s_xrh = sem("s_xrh")
        s_xrl = sem("s_xrl")
        s_xg = sem("s_xg")
        s_rt = sem("s_rt")
        s_scat = sem("s_scat")
        s_wld = [sem(f"s_wld{k}") for k in range(2)]
        s_wsh = sem("s_wsh")
        s_wsl = sem("s_wsl")
        s_wss = sem("s_wss")
        s_wst = [sem(f"s_wst{k}") for k in range(2)]
        s_ga = sem("s_ga")
        s_gi = sem("s_gi")
        s_mix = sem("s_mix")
        s_x2 = sem("s_x2")

        s_tab = sem("s_tab")
        s_tt = sem("s_tt")
        s_zf = sem("s_zf")
        s_rf = sem("s_rf")
        s_te = sem("s_te")
        s_mr = [sem(f"s_mr{k}") for k in range(2)]
        s_w13 = [sem(f"s_w13_{k}") for k in range(2)]
        s_w2 = [sem(f"s_w2_{k}") for k in range(2)]
        s_yst = [sem(f"s_yst{k}") for k in range(2)]
        s_xtp = sem("s_xtp")
        s_xt = sem("s_xt")
        s_h = sem("s_h")
        s_sg = sem("s_sg")
        s_hb = sem("s_hb")
        s_hh = sem("s_hh")
        s_hl = sem("s_hl")
        s_y = sem("s_y")
        s_ye = sem("s_ye")
        s_fw = sem("s_fw")
        s_fa = sem("s_fa")
        s_fr = sem("s_fr")
        s_ft = sem("s_ft")
        s_fq = sem("s_fq")
        s_xf = [sem(f"s_xf{k}") for k in range(4)]
        s_ost = [sem(f"s_ost{k}") for k in range(2)]
        s_f1 = sem("s_f1")
        s_f2 = sem("s_f2")
        s_fv = sem("s_fv")
        s_frs = sem("s_frs")
        s_q1 = sem("s_q1")
        s_q1p = sem("s_q1p")
        s_q1t = sem("s_q1t")
        s_gu = sem("s_gu")
        s_sil = sem("s_sil")
        s_hm = sem("s_hm")
        s_q2a = sem("s_q2a")
        s_q2 = sem("s_q2")
        s_q2p = sem("s_q2p")
        s_q2t = sem("s_q2t")
        s_dn = sem("s_dn")
        s_res = sem("s_res")
        RF_TDIF = 4 + 1 + E + 4 + 2 + 1 + 2 * (E - 1) + 1 + 2 + 1

        RT = 18
        xh, xl = xhl[:, 0], xhl[:, 1]

        with nc.Block() as block:
            wld = bigf[:, 0:4096].rearrange("p (l n) -> p l n", l=2)

            @block.sync
            def _(sp):
                for dst, src in ((gts[:], a["g"]), (gate[:], a["gate"]), (maskf[:], a["mask"]), (kpm8[:].bitcast(I32), a["kpm"]),
                                 (bqk[:], a["bqk"]), (bv[:], a["bv"]), (bo[:], a["bo"])):
                    sp.dma_start(dst, src).then_inc(s_set, 16)
                for l in range(2):
                    sp.dma_start(wld[:, l, :], a["aw"][l]).then_inc(s_setw, 16)
                sp.wait_ge(s_const, 4)
                for slot in range(3):
                    for ab in range(2):
                        sp.dma_start(ks[SHA:SHA + 2, slot, ab].rearrange("p a t -> p (a t)"), kconst[:, ab]).then_inc(s_krow, 16)
                sp.wait_ge(s_kpm, 1)
                sp.dma_start(kpm_d[0:B, :], kpmh[:]).then_inc(s_krow, 16)
                sp.dma_start(kpm_d[B:2 * B, :], zero16[0:B, 0, 0:S]).then_inc(s_krow, 16)
                sp.wait_ge(s_krow, 16 * 8)

            @block.gpsimd
            def _(pool):
                pool.memset(id32[:], 0.0)
                pool.memset(id16[:], 0.0)
                pool.memset(idb[:], 0.0)
                pool.memset(idmask[:], 0.0)
                pool.memset(lower[:], 0.0)
                pool.memset(ones16[:], 1.0)
                pool.memset(ones32[:], 1.0)
                pool.memset(kconst[:], 0.0).then_inc(s_id, 1)
                pool.wait_ge(s_id, 1)
                for t, v in ((id32, 1.0), (id16, 1.0), (idb, 1.0), (idmask, 1.0 / LOGIT)):
                    pool.affine_select(out=t[:], in_=t[:], compare_op=ALU.not_equal, fill=v, base=0,
                                       pattern=[[-1, P]], channel_multiplier=1)
                pool.affine_select(out=lower[:], in_=lower[:], compare_op=ALU.is_ge, fill=1.0, base=0,
                                   pattern=[[-1, P]], channel_multiplier=1)
                pool.affine_select(out=kconst[:], in_=kconst[:], compare_op=ALU.not_equal, fill=SHIFT, base=0,
                                   pattern=[[-1, 2], [0, PAIRS * S]], channel_multiplier=1)
                pool.iota(w8[:], [[-1, E]], base=E, channel_multiplier=0, allow_small_or_imprecise_dtypes=True)
                pool.iota(runb[:], [[REGION, E]], base=0, channel_multiplier=0, allow_small_or_imprecise_dtypes=True)
                pool.memset(mhalf[:], -0.5)
                pool.memset(zero[:], 0.0)
                pool.memset(zero16[:], 0.0).then_inc(s_const, 1)
                pool.memset(ks[:, :, :, :, :], 0.0).then_inc(s_const, 1)
                pool.wait_ge(s_const, 2)
                pool.memset(qs[KPM:KPM + 1, :, :, :], 1.0 / LOGIT).then_inc(s_const, 1)
                pool.wait_ge(s_const, 3)
                pool.memset(vv[:, :, :, :, HD + 1:32], 0.0)
                pool.memset(vv[:, :, :, :, HD:HD + 1], 1.0).then_inc(s_const, 1)

            @block.scalar
            def _(act):
                act.wait_ge(s_set, 7 * 16)
                act.activation(tg[:], gts[:], ACT.Tanh).then_inc(s_tg, 1)
                act.wait_ge(s_tg, 1)
                act.activation(tg64[:], tg[:], ACT.Copy, scale=1.0 / WSC)
                act.activation(gatehl[:, 0], gate[:], ACT.Copy, scale=WSC).then_inc(s_wh, 1)
                for l in range(2):
                    act.wait_ge(s_setw, 32)
                    act.activation(aw[:, l, 0].rearrange("p w c n -> p (w c n)"), wld[:, l, :], ACT.Copy, scale=WSC).then_inc(s_wh, 1)

            @block.vector
            def _(dve):
                dve.wait_ge(s_set, 7 * 16)
                dve.tensor_reduce(maxmask[:], maskf[:], X, ALU.max).then_inc(s_dset, 1)
                dve.wait_ge(s_dset, 1)
                for c in range(C2):
                    dve.tensor_scalar(maskf[:, c], maskf[:, c], maxmask[:, c:c + 1], MASKED, ALU.subtract, ALU.max).then_inc(s_dset, 1)
                dve.wait_ge(s_dset, 3)
                dve.tensor_copy(maskh[:], maskf[:]).then_inc(s_dset, 1)
                dve.tensor_scalar(kpmh[:], kpm8[:], MASKED, None, ALU.mult).then_inc(s_kpm, 1)
                dve.tensor_scalar(bqk[:], bqk[:], WSC, None, ALU.mult)
                dve.wait_ge(s_tg, 1)
                dve.tensor_scalar(bo[:], bo[:], tg[:, 2:3], None, ALU.mult)
                dve.wait_ge(s_wh, 1)
                dve.scalar_tensor_tensor(out=gatehl[:, 1], in0=gate[:], scalar=WSC, in1=gatehl[:, 0], op0=ALU.mult, op1=ALU.subtract)
                for l in range(2):
                    dve.wait_ge(s_wh, l + 2)
                    dve.scalar_tensor_tensor(out=aw[:, l, 1].rearrange("p w c n -> p (w c n)"), in0=wld[:, l, :], scalar=WSC,
                                             in1=aw[:, l, 0].rearrange("p w c n -> p (w c n)"), op0=ALU.mult, op1=ALU.subtract)
                dve.wait_ge(s_maskt, 1)
                dve.tensor_scalar(maskT[:], psM[:, :].rearrange("p (c n) -> p c n", c=C2), 1.0 / LOGIT, None, ALU.mult)

            @block.tensor
            def _(pe):
                pe.wait_ge(s_const, 1)
                pe.wait_ge(s_dset, 3)
                for kc in range(C2):
                    for qc in range(C2):
                        last = pe.transpose(psM[:, kc * S + qc * P:kc * S + (qc + 1) * P], maskf[:, qc, kc * P:(kc + 1) * P], id32[:])
                last.then_inc(s_maskt, 1)

        def attention(L):
            misc = Misc(L, 0 if L == 0 else Misc(0, 0).end)
            xsrc, xres, xdst = (a["x"], a["x"], x1_d) if L == 0 else (x1_d, x2_d, x3_d)
            FULL = (misc.first_full, misc.last_full)
            LAST = B + 3 if L == 0 else B + 2

            def batch_rows(d, b):
                return d[bass.ds(b * S, S)].rearrange("(c p) d -> p c d", p=P)

            def valid(i, lag):
                return not isinstance(i, int) or 0 <= i - lag < B

            def iterations(eng, body):
                for i in range(-1, FULL[0]):
                    body(i, i % 3, i // 3)
                with eng.Fori(0, (FULL[1] - FULL[0] + 1) // 3) as j:
                    for k in range(FULL[0], FULL[0] + 3):
                        body(j * 3 + k, k % 3, j + k // 3)
                for i in range(FULL[1] + 1, LAST):
                    body(i, i % 3, i // 3)

            def landed(r, q):
                slot, turn = (r + 1) % 3, (r + 1) // 3
                before = L * len(range(slot, B, 3))
                return q * 16 + 16 * (turn + before + 1)

            def splits(i):
                return L == 0 and (not isinstance(i, int) or 2 <= i < 2 + 3 * E // 2)

            def bank(name):
                return psN if name in Misc.SECOND else psM[:, :]

            def exps(b):
                return n(b) * 8 if L == 0 else n(b) * 16 - 8 * B

            def head_slot(r, s):
                return (r + 2 + s) % 3

            def piece(d, m):
                return d[bass.ds(m, 1)].rearrange("o p n -> (o p) n")

            def n(i, lag=0):
                return i + (L * B - lag)

            with nc.Block() as block:

                @block.sync
                def _(sp):
                    def load(i, slot):
                        if valid(i, 3):
                            sp.wait_ge(s_xn, 2 * n(i, 3) + 2)
                            apart(sp)
                            sp.wait_ge(s_cl, n(i, 3) + 1)
                            sp.wait_ge(s_ch, n(i, 3) + 1)
                        sp.dma_start(xin[:, slot], batch_rows(xsrc, i)).then_inc(s_x[slot], 16)
                        sp.dma_start(cin[:, slot], a["ctx"][bass.ds(i, 1)].rearrange("o p c n -> (o p) c n")).then_inc(s_c[slot], 16)

                    def shift(b, slot, half):
                        sp.wait_ge(s_mt, 2 * n(b) + 1 + half)
                        sp.dma_start(qs[SHA:SHA + 2, slot, 4 * half:4 * half + 4].rearrange("p a t -> p (a t)"), mt[:, half]).then_inc(s_sh, 16)

                    def body(i, r, q):
                        one, two = (r + 2) % 3, (r + 1) % 3
                        if isinstance(i, int) and i == -1:
                            load(0, 0)
                        if valid(i, 1):
                            shift(i - 1, one, 1)
                        if valid(i, -2):
                            load(i + 2, one)
                        if valid(i, 2):
                            if not isinstance(i, int) or i > 2:
                                sp.wait_ge(s_xst, 16 * n(i, 2))
                                apart(sp)
                                if L == 0:
                                    sp.wait_ge(s_xn1, 2 * (i - 2))
                            sp.dma_start(xo, batch_rows(xres, i - 2)).then_inc(s_xo, 16)
                        if valid(i, -1):
                            b = i + 1
                            if L == 1:
                                sp.wait_ge(s_mix, 4 * b + 4)
                                sp.dma_start(batch_rows(x2_d, b), xin[:, two]).then_inc(s_x2, 16)
                            if not isinstance(i, int) or i >= 2:
                                sp.wait_ge(s_t, 16 * (n(b) - 2))
                                apart(sp)
                            if L == 1 and isinstance(i, int) and i < 2:
                                sp.wait_ge(s_t, 16 * B)
                            sp.wait_ge(s_kh, n(b) + 1)
                            apart(sp)
                            sp.wait_ge(s_kl, n(b) + 1)
                            apart(sp)
                            for k, l in ((0, 0), (1, 0), (2, 1)):
                                for ab in range(2):
                                    sp.dma_start(ks[32 * k + 16 * ab:32 * k + 16 * ab + 16, two, ab].rearrange("p a t -> p (a t)"),
                                                 khl[64 * ab:64 * ab + 64, l]).then_inc(s_kst, 16)
                            for ab in range(2):
                                sp.dma_start(ks[KPM:KPM + 1, two, ab], kpm_d[bass.ds(n(b), 1)].unsqueeze(1).broadcast_to([1, PAIRS, S])).then_inc(s_kst, 16)
                            sp.wait_ge(s_qh, n(b) + 1)
                            sp.wait_ge(s_ql, n(b) + 1)
                            for k, l in ((0, 0), (1, 1), (2, 0)):
                                sp.dma_start(qs[32 * k:32 * k + 32, two].rearrange("p a t -> p (a t)"), qhl[:, l]).then_inc(s_qst, 16)
                            if L == 1:
                                sp.wait_ge(s_x2, 16 * b + 16)
                        if valid(i, 0):
                            shift(i, r, 0)
                        if valid(i, 2):
                            sp.wait_ge(s_x1, n(i, 2) + 1)
                            sp.dma_start(batch_rows(xdst, i - 2), xo).then_inc(s_xst, 16)
                        if L == 0 and isinstance(i, int) and i == 1:
                            for k in range(2):
                                sp.dma_start(wst[:, k], piece(a["moe"], k)).then_inc(s_wld[k], 16)
                        if splits(i):
                            for k in range(2):
                                m = (i - 2) * 2 + k
                                sp.wait_ge(s_wsl, m + 1)
                                sp.dma_start(piece(ws_d, m), wsp[:, k].rearrange("p l n -> p (l n)")).then_inc(s_wst[k], 16)
                                if not isinstance(i, int) or m + 2 < 3 * E:
                                    sp.dma_start(wst[:, k], piece(a["moe"], m + 2)).then_inc(s_wld[k], 16)

                    iterations(sp, body)
                    sp.wait_ge(s_xst, 16 * B * (L + 1))
                    if L == 0:
                        for k in range(2):
                            sp.wait_ge(s_wst[k], 16 * 3 * E // 2)
                        sp.wait_ge(s_scat, 64 * B)

                @block.gpsimd
                def _(pool):
                    def body(i, r, q):
                        two = (r + 1) % 3
                        if valid(i, -1):
                            b = i + 1
                            if L == 1:
                                if not isinstance(i, int) or i >= 0:
                                    pool.wait_ge(s_mix, 4 * b)
                                pool.tensor_copy(gidx[:].unsqueeze(1), POS[:, bass.ds(b, 1)]).then_inc(s_gi, 1)
                                pool.wait_ge(s_gi, b + 1)
                                apart(pool)
                                for k in range(2):
                                    for c in range(C2):
                                        pool.indirect_dma_start(ga[:, k, c], None, y_d[:, :],
                                                                bass.IndirectOffsetOnAxis(ap=gidx[:, 2 * k + c:2 * k + c + 1], axis=0)).then_inc(s_ga, 16)
                            pool.wait_ge(s_ln, 4 * n(b) + 4)
                            apart(pool)
                            pool.tensor_scalar(lnrs[:, 0], lnmv[:, :, 1], EPS, None, ALU.add).then_inc(s_var, 1)
                            pool.wait_ge(s_var, n(b) + 1)
                            pool.tensor_tensor(lnrs[:, 1], lnrs[:, 0], mhalf[:], ALU.pow).then_inc(s_rs, 1)
                            pool.wait_ge(s_ch, n(b) + 1)
                            pool.wait_ge(s_c[two], landed(r, q))
                            pool.tensor_tensor(chl[:, 1], cin[:, two], chl[:, 0], ALU.subtract).then_inc(s_cl, 1)
                        if splits(i):
                            for k in range(2):
                                m = (i - 2) * 2 + k
                                pool.wait_ge(s_wsh, m + 1)
                                pool.tensor_tensor(wsp[:, k, 1], wst[:, k], wsp[:, k, 0], ALU.subtract).then_inc(s_wsl, 1)
                        if L == 0 and valid(i, 2):
                            b = i - 2
                            pool.wait_ge(s_l2, 4 * b + 4)
                            apart(pool)
                            pool.tensor_scalar(l2rs[:, 0], l2mv[:, :, 1], EPS, None, ALU.add).then_inc(s_var2, 1)
                            pool.wait_ge(s_var2, b + 1)
                            pool.tensor_tensor(l2rs[:, 1], l2rs[:, 0], mhalf[:], ALU.pow).then_inc(s_rs2, 1)
                            pool.wait_ge(s_xrh, b + 1)
                            pool.tensor_tensor(xr[:, two, :, D:2 * D], xn1[:], xr[:, two, :, 0:D], ALU.subtract).then_inc(s_xrl, 1)
                        if L == 0 and valid(i, 3):
                            b = i - 3
                            pool.wait_ge(s_rt, RT * (b + 1))
                            apart(pool)
                            for k in range(2):
                                for c in range(C2):
                                    pool.indirect_dma_start(routed_d[:, :], bass.IndirectOffsetOnAxis(ap=rowi[:, k, c:c + 1], axis=0),
                                                            xr[:, r, c], None).then_inc(s_scat, 16)

                    iterations(pool, body)

                @block.scalar
                def _(act):
                    def body(i, r, q):
                        one, two = (r + 2) % 3, (r + 1) % 3
                        for s in range(16):
                            if s == 1 and valid(i, 2):
                                u_out(i - 2, 1)
                            if (s % 2 or L == 1) and valid(i, 1):
                                exp(i - 1, s, head_slot(r, s))
                            if s == 9 and valid(i, 1):
                                u_out(i - 1, 0)
                            if s == 0 and valid(i, 1):
                                maxima(i, i - 1, 1)
                            if s == 11 and valid(i, 0):
                                maxima(i, i, 0)
                            if s == 0 and valid(i, -1):
                                b = i + 1
                                act.wait_ge(s_c[two], landed(r, q))
                                if not isinstance(i, int) or i >= 0:
                                    act.wait_ge(s_md, misc.before(i - 1, "V") + 1)
                                act.activation(chl[:, 0], cin[:, two], ACT.Copy).then_inc(s_ch, 1)
                            if s == 5 and valid(i, -1):
                                act.wait_ge(s_md, misc.before(i, "XT") + 1)
                                act.activation(xh, psM[:, :].rearrange("p (c n) -> p c n", c=C2), ACT.Copy).then_inc(s_xh, 1)
                            for name, step, dst, done, copied, w in (("Q", 7, qhl, s_qh, s_qst, 48), ("K", 2, khl, s_kh, s_kst, 128)):
                                if s == step and valid(i, -1):
                                    act.wait_ge(s_md, misc.before(i, name) + 1)
                                    if not isinstance(i, int) or i >= 0:
                                        act.wait_ge(copied, w * n(i, -1))
                                    if L == 0:
                                        act.activation(dst[:, 0], bank(name), ACT.Copy).then_inc(done, 1)
                                    else:
                                        for g in range(C2):
                                            last = act.activation(dst[:, 0, g * S:(g + 1) * S], bank(name)[:, g * S:(g + 1) * S], ACT.Identity,
                                                                  bias=bqk[:, int(name == "K"), g:g + 1])
                                        last.then_inc(done, 1)
                            if s in (3, 6) and splits(i):
                                k = s // 6
                                act.wait_ge(s_wld[k], 16 * (i - 1))
                                act.activation(wst[:, k], wst[:, k], ACT.Copy, scale=WSC).then_inc(s_wss, 1)
                            if s in (4, 9) and splits(i):
                                k = s // 9
                                act.wait_ge(s_wss, (i - 2) * 2 + k + 1)
                                if not isinstance(i, int) or i > 2:
                                    act.wait_ge(s_wst[k], 16 * (i - 2))
                                act.activation(wsp[:, k, 0], wst[:, k], ACT.Copy).then_inc(s_wsh, 1)
                            if s == 8 and valid(i, 2):
                                act.wait_ge(s_md, misc.before(i, "OT") + 1)
                                act.activation(ohl[:, 0], psN.rearrange("p (c n) -> p c n", c=C2), ACT.Copy).then_inc(s_oh, 1)
                            if L == 0 and s == 14 and valid(i, 2):
                                b = i - 2
                                act.wait_ge(s_xn1, 2 * b + 2)
                                act.activation(xr[:, two, :, 0:D], xn1[:], ACT.Copy).then_inc(s_xrh, 1)
                            if L == 0 and s == 1 and valid(i, 3):
                                act.wait_ge(s_md, misc.before(i, "GT") + 1)
                                act.activation(xg[:].rearrange("p k n -> p (k n)"), psM16, ACT.Copy).then_inc(s_xg, 1)

                    def maxima(i, b, half):
                        act.wait_ge(s_md, misc.before(i, f"M{half}") + 1)
                        if not isinstance(b, int) or n(b) > 0:
                            act.wait_ge(s_sh, 32 * n(b) - 16 + 16 * half)
                        act.activation(mt[:, half], bank(f"M{half}")[0:8, 0:S], ACT.Copy, scale=-1.0 / SHIFT).then_inc(s_mt, 1)

                    def exp(b, s, slot):
                        p = s // 2
                        if L == 0:
                            act.wait_ge(s_add, 16 * b + s + 1)
                            act.activation(pt[:, p % 4], pt[:, p % 4], ACT.Exp, scale=LOGIT).then_inc(s_exp, 1)
                        else:
                            act.wait_ge(s_t, 16 * n(b) + s + 1)
                            if s % 2 == 0:
                                act.wait_ge(s_pv, 4 * n(b) + p // 2 - 1)
                            act.activation(pt[:, p % 4, s % 2], psH[:, slot], ACT.Exp, scale=LOGIT).then_inc(s_exp, 1)

                    def u_out(b, half):
                        act.wait_ge(s_pv, 4 * n(b) + 2 * half + 2)
                        if half == 0 and (not isinstance(b, int) or b > 0):
                            act.wait_ge(s_o, 2 * n(b))
                        act.activation(uu[:, half], psU[:, :], ACT.Copy).then_inc(s_u, 1)

                    iterations(act, body)

                @block.vector
                def _(dve):
                    def stats(src, st, mv, done, m):
                        for c in range(C2):
                            dve.bn_stats(st[:, c], src[:, c]).then_inc(done, 1)
                        for c in range(C2):
                            dve.wait_ge(done, 4 * m + c + 1)
                            apart(dve)
                            dve.bn_aggr(mv[:, c], st[:, c]).then_inc(done, 1)

                    def body(i, r, q):
                        one, two = (r + 2) % 3, (r + 1) % 3
                        b = i + 1
                        for s in range(16):
                            if valid(i, 0):
                                half, col = s // 8, (s % 2) * 4 + (s % 8) // 2
                                dve.wait_ge(s_s, 16 * n(i) + s + 1)
                                if s % 8 == 0 and (not isinstance(i, int) or i > 0):
                                    dve.wait_ge(s_mt, 2 * n(i) - 1 + half)
                                dve.tensor_reduce(mx[:, half, :, col], psS[:, s % 2].rearrange("p (c n) -> p c n", c=C2), X, ALU.max).then_inc(s_mx, 1)
                            if L == 0 and 4 <= s < 11 and valid(i, 3):
                                choose(i, i - 3, 2 * (s - 4))
                            if L == 0 and valid(i, 1):
                                p = s // 2
                                dve.wait_ge(s_t, 16 * (i - 1) + s + 1)
                                if s % 2 == 0 and (not isinstance(i, int) or 4 * (i - 1) + p // 2 > 1):
                                    dve.wait_ge(s_pv, 4 * (i - 1) + p // 2 - 1)
                                dve.tensor_tensor(pt[:, p % 4, s % 2], psH[:, head_slot(r, s)], maskT[:].rearrange("p c n -> p (c n)"), ALU.add).then_inc(s_add, 1)
                            if L == 0 and 4 <= s < 10 and valid(i, 3):
                                choose(i, i - 3, 2 * (s - 4) + 1)
                            if s == 0 and valid(i, -1):
                                dve.wait_ge(s_x[two], landed(r, q))
                                if L == 1:
                                    for k in range(2):
                                        for c in range(C2):
                                            if k == 0 and c == 0:
                                                dve.wait_ge(s_ga, 64 * b + 64)
                                            if k == 1:
                                                dve.wait_ge(s_mix, 4 * b + c + 1)
                                            dve.scalar_tensor_tensor(out=xin[:, two, c], in0=ga[:, k, c], scalar=WAB[:, k, bass.ds(b * 2 + c, 1)],
                                                                     in1=xin[:, two, c], op0=ALU.mult, op1=ALU.add).then_inc(s_mix, 1)
                                    dve.wait_ge(s_mix, 4 * b + 4)
                                stats(xin[:, two], lnst, lnmv, s_ln, n(b))
                            if s == 3 and valid(i, -1):
                                dve.wait_ge(s_rs, n(b) + 1)
                                for c in range(C2):
                                    dve.tensor_scalar(xn[:, c], xin[:, two, c], lnmv[:, c, 0:1], lnrs[:, 1, c:c + 1], ALU.subtract, ALU.mult).then_inc(s_xn, 1)
                            if s == 13 and L == 0 and valid(i, 3):
                                rows_of(i, i - 3)
                            if s == 6 and valid(i, -1):
                                dve.wait_ge(s_xh, n(b) + 1)
                                dve.tensor_tensor(xl, psM[:, :].rearrange("p (c n) -> p c n", c=C2), xh, ALU.subtract).then_inc(s_xl, 1)
                            for qc in range(2):
                                if s == 5 + 2 * qc and valid(i, 2):
                                    dve.wait_ge(s_md, misc.before(i, f"UT{qc}") + 1)
                                    heads = psN.rearrange("p (h k) -> p h k", k=32)
                                    dve.reciprocal(rden[:, qc], heads[:, :, HD]).then_inc(s_rd, 1)
                                    dve.wait_ge(s_rd, 2 * n(i, 2) + qc + 1)
                                    ins = dve.tensor_tensor(oo[:, qc].rearrange("p (h k) -> p h k", k=HD), heads[:, :, 0:HD],
                                                            rden[:, qc].unsqueeze(2).broadcast_to([P, H, HD]), ALU.mult)
                                    ins.then_inc(s_o, 1)
                            for name, step, dst, done, high in (("Q", 8, qhl, s_ql, s_qh), ("K", 3, khl, s_kl, s_kh)):
                                if s == step and valid(i, -1):
                                    dve.wait_ge(high, n(b) + 1)
                                    if L == 0:
                                        dve.tensor_tensor(dst[:, 1], bank(name), dst[:, 0], ALU.subtract).then_inc(done, 1)
                                    else:
                                        for g in range(C2):
                                            last = dve.scalar_tensor_tensor(out=dst[:, 1, g * S:(g + 1) * S], in0=bank(name)[:, g * S:(g + 1) * S],
                                                                            scalar=bqk[:, int(name == "K"), g:g + 1],
                                                                            in1=dst[:, 0, g * S:(g + 1) * S], op0=ALU.add, op1=ALU.subtract)
                                        last.then_inc(done, 1)
                            if s == 9 and valid(i, 2):
                                dve.wait_ge(s_oh, n(i, 2) + 1)
                                dve.tensor_tensor(ohl[:, 1], psN.rearrange("p (c n) -> p c n", c=C2), ohl[:, 0], ALU.subtract).then_inc(s_ol, 1)
                            if s == 10 and valid(i, -1):
                                dve.wait_ge(s_md, misc.before(i, "V") + 1)
                                if not isinstance(i, int) or i >= 2:
                                    dve.wait_ge(s_pv, 4 * (n(b) - 2))
                                for c in range(C2):
                                    last = dve.scalar_tensor_tensor(out=vv[:, two, c, :, 0:HD], in0=psM[:, c * S:(c + 1) * S].rearrange("p (h k) -> p h k", k=HD),
                                                                    scalar=1.0 / WSC, in1=(bv if L else zero)[:].rearrange("p (h k) -> p h k", k=HD),
                                                                    op0=ALU.mult, op1=ALU.add)
                                last.then_inc(s_v, 1)
                            if s == 11 and valid(i, 2):
                                m = n(i, 2)
                                dve.wait_ge(s_xo, 16 * m + 16)
                                if L == 1:
                                    for c in range(C2):
                                        last = dve.tensor_tensor(xo[:, c], xo[:, c], bo[:], ALU.add)
                                    last.then_inc(s_bo, 1)
                                    dve.wait_ge(s_bo, i - 1)
                                dve.wait_ge(s_md, misc.before(i, "WO") + 1)
                                dve.scalar_tensor_tensor(out=xo[:], in0=psN.rearrange("p (c n) -> p c n", c=C2), scalar=tg64[:, 2 * L:2 * L + 1],
                                                         in1=xo[:], op0=ALU.mult, op1=ALU.add).then_inc(s_x1, 1)
                                if L == 0:
                                    dve.wait_ge(s_x1, m + 1)
                                    stats(xo, l2st, l2mv, s_l2, i - 2)
                            if s == 13 and L == 0 and valid(i, 2):
                                dve.wait_ge(s_rs2, i - 1)
                                if not isinstance(i, int) or i > 2:
                                    dve.wait_ge(s_xrl, i - 2)
                                for c in range(C2):
                                    dve.tensor_scalar(xn1[:, c], xo[:, c], l2mv[:, c, 0:1], l2rs[:, 1, c:c + 1], ALU.subtract, ALU.mult).then_inc(s_xn1, 1)

                    def choose(i, b, k):
                        wide = [P, C2, E]
                        w8b = w8[:].unsqueeze(1).broadcast_to(wide)
                        if k == 0:
                            dve.wait_ge(s_md, misc.before(i, "GS") + 1)
                            ins = dve.tensor_scalar(sc[:, 0], psM[:, 0:C2 * E].rearrange("p (c e) -> p c e", c=C2), 1.0 / WSC, None, ALU.mult)
                        else:
                            dve.wait_ge(s_rt, RT * b + k)
                            rnd_, part_ = (k - 1) // 6, (k - 1) % 6
                            if k == 12:
                                dve.tensor_copy(OH[:, bass.ds(b, 1)], oh[:].rearrange("p k c e -> p (k c e)").unsqueeze(1))
                                dve.tensor_copy(TOP[:, bass.ds(b, 1)], top[:].rearrange("p k c -> p (k c)").unsqueeze(1))
                                ins = dve.tensor_tensor(chosen[:], oh[:, 0], oh[:, 1], ALU.add)
                            elif part_ == 0:
                                ins = dve.tensor_reduce(top[:, rnd_], sc[:, rnd_], X, ALU.max)
                            elif part_ == 1:
                                ins = dve.tensor_tensor(eqm[:], sc[:, rnd_], top[:, rnd_].unsqueeze(2).broadcast_to(wide), ALU.is_equal)
                            elif part_ == 2:
                                ins = dve.tensor_tensor(eqm[:], eqm[:], w8b, ALU.mult)
                            elif part_ == 3:
                                ins = dve.tensor_reduce(wmax[:], eqm[:], X, ALU.max)
                            elif part_ == 4:
                                ins = dve.tensor_tensor(oh[:, rnd_], w8b, wmax[:].unsqueeze(2).broadcast_to(wide), ALU.is_equal)
                            else:
                                ins = dve.scalar_tensor_tensor(out=sc[:, 1], in0=oh[:, 0], scalar=-1e30, in1=sc[:, 0], op0=ALU.mult, op1=ALU.add)
                        ins.then_inc(s_rt, 1)

                    def rows_of(i, b):
                        dve.wait_ge(s_md, misc.before(i, "RK") + 1)
                        base = RT * b + 13
                        dve.tensor_tensor(rank[:], psN[:, 0:C2 * E].rearrange("p (c e) -> p c e", c=C2), runb[:].unsqueeze(1).broadcast_to([P, C2, E]), ALU.add).then_inc(s_rt, 1)
                        dve.wait_ge(s_rt, base + 1)
                        for k in range(2):
                            last = dve.tensor_tensor(prod[:, k], oh[:, k], rank[:], ALU.mult)
                        last.then_inc(s_rt, 1)
                        dve.tensor_tensor(runb[:], psN[:, C2 * E:C2 * E + E], runb[:], ALU.add).then_inc(s_rt, 1)
                        dve.wait_ge(s_rt, base + 3)
                        dve.tensor_reduce(row[:], prod[:], X, ALU.add).then_inc(s_rt, 1)
                        dve.wait_ge(s_rt, base + 4)
                        if not isinstance(i, int) or b > 0:
                            dve.wait_ge(s_scat, 64 * b)
                        dve.tensor_copy(ROW[:, bass.ds(b, 1)], row[:].rearrange("p k c -> p (k c)").unsqueeze(1))
                        dve.tensor_copy(rowi[:], row[:]).then_inc(s_rt, 1)

                    iterations(dve, body)

                @block.tensor
                def _(pe):
                    def proj(dst, stat, mov):
                        for c in range(C2):
                            for ls, lm in ((0, 0), (0, 1), (1, 0)):
                                last = pe.matmul(dst, stat(ls, c), mov(lm, c), start=(c == 0 and (ls, lm) == (0, 0)), stop=(c == C2 - 1 and ls == 1))
                        return last

                    def free(i, name):
                        front = misc.previous(i, name)
                        if front is None:
                            return
                        k, name = front
                        m = k - misc.lag[name]
                        done, value = {
                            "M0": (s_mt, 2 * n(m) + 1), "M1": (s_mt, 2 * n(m) + 2), "XT": (s_xl, n(m) + 1),
                            "UT0": (s_o, 2 * n(m) + 1), "UT1": (s_o, 2 * n(m) + 2), "Q": (s_ql, n(m) + 1), "K": (s_kl, n(m) + 1),
                            "V": (s_v, n(m) + 1), "OT": (s_ol, n(m) + 1), "WO": (s_x1, n(m) + 1), "GT": (s_xg, n(m) + 1),
                            "GS": (s_rt, RT * m + 1), "RK": (s_rt, RT * m + 16),
                        }[name]
                        pe.wait_ge(done, value)

                    def pv(b, g, slot):
                        pe.wait_ge(s_exp, exps(b) + (2 * g + 2) * (L + 1))
                        pe.wait_ge(s_v, n(b) + 1)
                        if g % 2 == 0 and (not isinstance(b, int) or n(b) > 0 or g > 0):
                            pe.wait_ge(s_u, 2 * n(b) + g // 2)
                        for kc in range(C2):
                            for j in range(4):
                                h = 4 * g + j
                                last = pe.matmul(psU[32 * j:32 * j + 32, (g % 2) * S:(g % 2 + 1) * S], vv[:, slot, kc, h],
                                                 pt[:, (h // 2) % 4, h % 2, kc * S:(kc + 1) * S], start=(kc == 0), stop=(kc == C2 - 1))
                        last.then_inc(s_pv, 1)

                    def body(i, r, q):
                        one, two = (r + 2) % 3, (r + 1) % 3
                        b = i + 1
                        for s in range(16):
                            h, p = s, s // 2
                            if valid(i, 0):
                                if s == 0:
                                    pe.wait_ge(s_qst, 48 * n(i) + 48)
                                    pe.wait_ge(s_kst, 128 * n(i) + 128)
                                if not isinstance(i, int) or 16 * n(i) + s > 1:
                                    pe.wait_ge(s_mx, 16 * n(i) + s - 1)
                                if L == 0:
                                    pe.matmul(psS[:, s % 2], idmask[:], maskh[:].rearrange("p c n -> p (c n)"), start=True, stop=False, skip_group_check=True)
                                for qc in range(C2):
                                    last = pe.matmul(psS[:, s % 2, qc * S:(qc + 1) * S], qs[0:SHA, r, p, qc * P:(qc + 1) * P], ks[0:SHA, r, s % 2, p],
                                                     start=(L == 1), stop=True, skip_group_check=True)
                                last.then_inc(s_s, 1)
                            if valid(i, 1):
                                if s % 8 == 0:
                                    pe.wait_ge(s_sh, 32 * n(i, 1) + 16 + 16 * (s // 8))
                                if L == 0:
                                    if not isinstance(i, int) or 16 * (i - 1) + s > 2:
                                        pe.wait_ge(s_add, 16 * (i - 1) + s - 2)
                                elif not isinstance(i, int) or 16 * (i - 1) + s > 2:
                                    pe.wait_ge(s_exp, exps(i - 1) + s - 2)
                                for kc in range(C2):
                                    last = pe.matmul(psH[:, head_slot(r, s), kc * S:(kc + 1) * S], ks[0:STACK, one, s % 2, p, kc * P:(kc + 1) * P],
                                                     qs[0:STACK, one, p], start=True, stop=True)
                                last.then_inc(s_t, 1)
                            if s == 1 and valid(i, 2):
                                pv(i - 2, 3, two)
                            if s in (5, 9, 13) and valid(i, 1):
                                pv(i - 1, s // 4 - 1, one)
                            name = misc.steps.get(s)
                            if name is None or not valid(i, misc.lag[name]):
                                continue
                            free(i, name)
                            if name in ("M0", "M1"):
                                half, m = int(name[1]), i - misc.lag[name]
                                pe.wait_ge(s_mx, 16 * n(m) + 8 * half + 8)
                                for qc in range(C2):
                                    last = pe.transpose(bank(name)[0:8, qc * P:(qc + 1) * P], mx[:, half, qc], id32[:])
                            elif name == "XT":
                                pe.wait_ge(s_xn, 2 * n(b) + 2)
                                for c in range(C2):
                                    for t in range(C2):
                                        last = pe.transpose(psM[:, c * S + t * P:c * S + (t + 1) * P], xn[:, t, c * P:(c + 1) * P], id32[:])
                            elif name == "Q":
                                pe.wait_ge(s_xl, n(b) + 1)
                                for g in range(C2):
                                    last = proj(psM[:, g * S:(g + 1) * S], lambda l, c: aw[:, L, l, 0, c, g * P:(g + 1) * P], lambda l, c: xhl[:, l, c])
                            elif name == "K":
                                pe.wait_ge(s_cl, n(b) + 1)
                                for g in range(C2):
                                    last = proj(psN[:, g * S:(g + 1) * S], lambda l, c: aw[:, L, l, 1, c, g * P:(g + 1) * P], lambda l, c: chl[:, l, c])
                            elif name == "V":
                                for t in range(C2):
                                    last = proj(psM[:, t * S:(t + 1) * S], lambda l, c: chl[:, l, c, t * P:(t + 1) * P], lambda l, c: aw[:, L, l, 2, c])
                            elif name in ("UT0", "UT1"):
                                qc = int(name[2])
                                pe.wait_ge(s_u, 2 * n(i, 2) + 2)
                                for g in range(4):
                                    last = pe.transpose(psN[:, g * P:(g + 1) * P], uu[:, g // 2, (g % 2) * S + qc * P:(g % 2) * S + (qc + 1) * P], id32[:])
                            elif name == "OT":
                                pe.wait_ge(s_o, 2 * n(i, 2) + 2)
                                for c in range(C2):
                                    for t in range(C2):
                                        last = pe.transpose(psN[:, c * S + t * P:c * S + (t + 1) * P], oo[:, t, c * P:(c + 1) * P], id32[:])
                            elif name == "WO":
                                pe.wait_ge(s_ol, n(i, 2) + 1)
                                for t in range(C2):
                                    last = proj(psN[:, t * S:(t + 1) * S], lambda l, c: ohl[:, l, c, t * P:(t + 1) * P], lambda l, c: aw[:, L, l, 3, c])
                            elif name == "GT":
                                pe.wait_ge(s_xrl, i - 2)
                                for l in range(2):
                                    for c in range(C2):
                                        for t in range(C2):
                                            at_ = (2 * l + c) * S + t * P
                                            last = pe.transpose(psM16[:, at_:at_ + P], xr[:, r, t, l * D + c * P:l * D + (c + 1) * P], id16[:])
                            elif name == "GS":
                                pe.wait_ge(s_xg, i - 2)
                                for t in range(C2):
                                    last = proj(psM[:, t * E:(t + 1) * E], lambda l, c: xg[:, 2 * l + c, t * P:(t + 1) * P], lambda l, c: gatehl[:, l, c])
                            elif name == "RK":
                                pe.wait_ge(s_rt, RT * (i - 3) + 13)
                                pe.matmul(psN[:, 0:E], lower[:], chosen[:, 0], start=True, stop=True)
                                pe.matmul(psN[:, E:2 * E], lower[:], chosen[:, 1], start=True, stop=False)
                                pe.matmul(psN[:, E:2 * E], ones16[:], chosen[:, 0], start=False, stop=True)
                                pe.matmul(psN[:, 2 * E:3 * E], ones16[:], chosen[:, 0], start=True, stop=False)
                                last = pe.matmul(psN[:, 2 * E:3 * E], ones16[:], chosen[:, 1], start=False, stop=True)
                            last.then_inc(s_md, 1)

                    iterations(pe, body)

        attention(0)

        with nc.Block() as block:
            w13 = big[:, :, 0:2].rearrange("p s w l (c n) -> p s w l c n", c=C2)
            w2 = big[:, :, 2].rearrange("p s l (c n) -> p s l c n", c=NI)

            @block.sync
            def _(sp):
                sp.wait_ge(s_tab, 1)
                for e in range(E):
                    first = sp.value_load(endi[0:1, e:e + 1], min_val=0, max_val=E * REGION - TILE)
                    sp.dma_start(routed_d[bass.ds(first, TILE)].rearrange("(c p) n -> p c n", p=P), zero16[:]).then_inc(s_zf, 16)

                def rows(t, slot):
                    first = sp.value_load(rowt[0:1, bass.ds(t, 1)], min_val=0, max_val=E * REGION - TILE)
                    sp.dma_start(mxr[:, slot], routed_d[bass.ds(first, TILE)].rearrange("(c p) n -> p c n", p=P)).then_inc(s_mr[slot], 16)

                def weights(t, slot, js):
                    e3 = sp.value_load(eidt[0:1, bass.ds(t, 1)], min_val=0, max_val=3 * E - 3)
                    for j in js:
                        sp.dma_start(big[:, slot, j].rearrange("p l n -> p (l n)"), ws_d[bass.ds(e3 + j, 1)].rearrange("o p n -> (o p) n")).then_inc((s_w2 if j == 2 else s_w13)[slot], 16)

                def tile(t, slot, more=True):
                    if more:
                        sp.wait_ge(s_xtp, t + 1)
                        rows(t + 2, slot)
                        sp.wait_ge(s_h, 4 * t + 4)
                        apart(sp)
                        weights(t + 2, slot, (0, 1))
                    sp.wait_ge(s_ye, t + 1)
                    sp.dma_start(y_d[bass.ds(t * TILE, TILE)].rearrange("(c p) d -> p c d", p=P), ye[:, slot].rearrange("p (c d) -> p c d", c=C2)).then_inc(s_yst[slot], 16)
                    if more:
                        weights(t + 2, slot, (2,))

                for t in range(2):
                    weights(t, t, (0, 1))
                    if t == 0:
                        sp.wait_ge(s_zf, 16 * E)
                    rows(t, t)
                    weights(t, t, (2,))
                for t in range(3):
                    tile(t, t % 2)
                with sp.Fori(0, (NT - 5) // 2) as j:
                    for r in range(2):
                        tile(j * 2 + (3 + r), (3 + r) % 2)
                for t in range(NT - 2, NT):
                    tile(t, t % 2, more=False)
                for slot in range(2):
                    sp.wait_ge(s_yst[slot], 16 * len(range(slot, NT, 2)))

            @block.gpsimd
            def _(pool):
                pool.iota(tt[:], [[1, NT]], base=0, channel_multiplier=0, allow_small_or_imprecise_dtypes=True).then_inc(s_tt, 1)
                for k in range(3):
                    if k:
                        pool.wait_ge(s_fq, k)
                    pool.dma_start(fst[:], a["fw"][k]).then_inc(s_fw, 16)

            @block.vector
            def _(dve):
                k = [0]

                def step(ins):
                    k[0] += 1
                    ins.then_inc(s_rf, 1)
                    dve.wait_ge(s_rf, k[0])

                dve.tensor_copy(endi[:], runb[:])
                for e in range(E):
                    last = dve.tensor_scalar(cnt[:, e:e + 1], runb[:, e:e + 1], -float(e * REGION), None, ALU.add)
                step(last)
                step(dve.tensor_scalar(ntile[:], cnt[:], 1.0 / TILE, 0.5 - 0.5 / TILE, ALU.mult, ALU.add))
                step(dve.tensor_scalar(ntile[:], ntile[:], RND, None, ALU.add))
                step(dve.tensor_scalar(ntile[:], ntile[:], RND, None, ALU.subtract))
                step(dve.memset(cum[:], 0.0))
                for e in range(E):
                    step(dve.tensor_tensor(cum[:, e + 1:e + 2], cum[:, e:e + 1], ntile[:, e:e + 1], ALU.add))
                step(dve.tensor_scalar(base[:], cum[:, 0:E], -float(TILE), None, ALU.mult))
                for e in range(1, E):
                    last = dve.tensor_scalar(base[:, e:e + 1], base[:, e:e + 1], float(e * REGION), None, ALU.add)
                step(last)
                step(dve.tensor_scalar(delta[:], base[:], -1.0, None, ALU.mult))
                step(dve.tensor_tensor(dbase[:], base[:, 1:E], base[:, 0:E - 1], ALU.subtract))
                step(dve.tensor_scalar(lim[:], ntile[:, E - 1:E], -1.0, 0.0, ALU.add, ALU.max))
                step(dve.tensor_scalar(lim[:], lim[:], float(TILE), float((E - 1) * REGION), ALU.mult, ALU.add))
                dve.wait_ge(s_tt, 1)
                dve.memset(eid[:], 0.0)
                step(dve.tensor_scalar(rowf[:], tt[:], float(TILE), None, ALU.mult))
                for e in range(E - 1):
                    step(dve.tensor_scalar(ge[:], tt[:], cum[:, e + 1:e + 2], None, ALU.is_ge))
                    dve.tensor_tensor(eid[:], eid[:], ge[:], ALU.add)
                    step(dve.scalar_tensor_tensor(out=rowf[:], in0=ge[:], scalar=dbase[:, e:e + 1], in1=rowf[:], op0=ALU.mult, op1=ALU.add))
                step(dve.tensor_scalar(rowf[:], rowf[:], lim[:, 0:1], None, ALU.min))
                dve.tensor_copy(rowt[:], rowf[:])
                dve.tensor_scalar(eidt[:], eid[:], 3.0, None, ALU.mult).then_inc(s_tab, 1)
                wide = OH[:, :, :].rearrange("p b k -> p (b k)").rearrange("p (n e) -> p n e", e=E)
                step(dve.tensor_tensor(wide, wide, delta[:].unsqueeze(1).broadcast_to([P, 4 * B, E]), ALU.mult))
                step(dve.tensor_reduce(posf[:], wide, X, ALU.add))
                rows_ = ROW[:, :, :].rearrange("p b k -> p (b k)")
                dve.tensor_tensor(POS[:, :, :].rearrange("p b k -> p (b k)"), posf[:], rows_, ALU.add)
                tops = TOP[:, :, :].rearrange("p b (k c) -> p k b c", k=2)
                step(dve.tensor_tensor(tdif[:].rearrange("p (b c) -> p b c", c=C2), tops[:, 1], tops[:, 0], ALU.subtract))
                dve.wait_ge(s_te, 1)
                step(dve.tensor_scalar(tsum[:], tdif[:], 1.0, None, ALU.add))
                step(dve.reciprocal(tsum[:], tsum[:]))
                step(dve.tensor_scalar(WAB[:, 0], tsum[:], tg[:, 1:2], None, ALU.mult))
                dve.tensor_tensor(WAB[:, 1], WAB[:, 0], tdif[:], ALU.mult)

                def turned(t, slot):
                    dve.wait_ge(s_xtp, t + 1)
                    dve.tensor_copy(mxt[:, slot].rearrange("p k n -> p (k n)"), psM16).then_inc(s_xt, 1)

                def tile(t, slot, weight=False, last=False):
                    for p in range(4):
                        if weight and p == 1:
                            magnitudes(t)
                        dve.wait_ge(s_sg, 4 * t + p + 1)
                        dve.scalar_tensor_tensor(out=hb[:, p % 2], in0=psT[:, p % 2, 1], scalar=1.0 / WSC, in1=sg[:, p % 2], op0=ALU.mult, op1=ALU.mult).then_inc(s_hb, 1)
                        dve.wait_ge(s_hh, 4 * t + p + 1)
                        dve.tensor_tensor(hhl[:, slot, 1, 2 * p:2 * p + 2].rearrange("p c n -> p (c n)"), hb[:, p % 2],
                                          hhl[:, slot, 0, 2 * p:2 * p + 2].rearrange("p c n -> p (c n)"), ALU.subtract).then_inc(s_hl, 1)
                        if p == 2 and not last:
                            turned(t + 1, 1 - slot)
                        if weight and p > 1:
                            ternary(t, p - 2)

                def magnitudes(k):
                    dve.wait_ge(s_fw, 16 * k + 16)
                    dve.tensor_reduce(fabs[:, k:k + 1], fst[:], X, ALU.add, apply_absolute_value=True).then_inc(s_fa, 1)

                def ternary(k, half):
                    f = [3 * half]

                    def step(ins):
                        f[0] += 1
                        ins.then_inc(s_ft, 1)
                        dve.wait_ge(s_ft, 6 * k + f[0])
                    if half == 0:
                        dve.wait_ge(s_fr, k + 1)
                        step(dve.tensor_scalar(fmean[:, k:k + 1], psU[:, k:k + 1], 1.0 / (P * 2048), EPS, ALU.mult, ALU.max))
                        step(dve.reciprocal(fscale[:, k:k + 1], fmean[:, k:k + 1]))
                        step(dve.tensor_scalar(fst[:], fst[:], fscale[:, k:k + 1], RND, ALU.mult, ALU.add))
                        return
                    step(dve.tensor_scalar(fst[:], fst[:], RND, 1.0, ALU.subtract, ALU.min))
                    step(dve.tensor_scalar(fwt[:, k], fst[:], -1.0, None, ALU.max))
                    step(dve.tensor_scalar(fdeq[:, k:k + 1], fmean[:, k:k + 1], 1.0 / 127.0, None, ALU.mult))
                    dve.sem_inc(s_fq, 1)

                turned(0, 0)
                for t in range(3):
                    tile(t, t % 2, weight=True)
                with dve.Fori(0, (NT - 5) // 2) as j:
                    for r in range(2):
                        tile(j * 2 + (3 + r), (3 + r) % 2)
                for t in range(NT - 2, NT):
                    tile(t, t % 2, last=t == NT - 1)

            @block.scalar
            def _(act):
                act.wait_ge(s_rf, RF_TDIF)
                act.activation(tdif[:], tdif[:], ACT.Exp).then_inc(s_te, 1)

                def tile(t, slot, first=False):
                    for p in range(4):
                        act.wait_ge(s_h, 4 * t + p + 1)
                        if not (first and p < 2):
                            act.wait_ge(s_hb, 4 * t + p - 1)
                        act.activation(sg[:, p % 2], psT[:, p % 2, 0], ACT.Silu, scale=1.0 / WSC).then_inc(s_sg, 1)
                        act.wait_ge(s_hb, 4 * t + p + 1)
                        if p == 0 and (not isinstance(t, int) or t > 1):
                            act.wait_ge(s_y, t - 1)
                        act.activation(hhl[:, slot, 0, 2 * p:2 * p + 2].rearrange("p c n -> p (c n)"), hb[:, p % 2], ACT.Copy).then_inc(s_hh, 1)
                        if p == 1 and (not isinstance(t, int) or t > 0):
                            out_tile(t - 1, 1 - slot)

                def out_tile(t, slot):
                    act.wait_ge(s_y, t + 1)
                    if not isinstance(t, int) or t > 1:
                        act.wait_ge(s_yst[slot], yturn(t, slot))
                    act.activation(ye[:, slot], psS[:, slot], ACT.Copy, scale=1.0 / WSC).then_inc(s_ye, 1)

                turn = [0]

                def yturn(t, slot):
                    if isinstance(t, int):
                        return 16 * (t // 2)
                    return turn[0]

                for t in range(3):
                    tile(t, t % 2, first=t == 0)
                with act.Fori(0, (NT - 3) // 2) as j:
                    for r in range(2):
                        turn[0] = (j + 1) * 16
                        tile(j * 2 + (3 + r), (3 + r) % 2)
                out_tile(NT - 1, (NT - 1) % 2)

            @block.tensor
            def _(pe):
                def turned(t, slot):
                    pe.wait_ge(s_mr[slot], mturn(t))
                    if not isinstance(t, int) or t > 0:
                        pe.wait_ge(s_xt, t)
                    for l in range(2):
                        for c in range(C2):
                            for h in range(C2):
                                at_ = (2 * l + c) * TILE + h * P
                                last = pe.transpose(psM16[:, at_:at_ + P], mxr[:, slot, h, l * D + c * P:l * D + (c + 1) * P], id16[:])
                    last.then_inc(s_xtp, 1)

                jv = [None]

                def mturn(t):
                    if isinstance(t, int):
                        return 16 * (t // 2 + 1)
                    return jv[0]

                def first_products(t, slot, p):
                    if p == 0:
                        pe.wait_ge(s_xt, t + 1)
                        pe.wait_ge(s_w13[slot], wturn(t) * 2)
                    if not isinstance(t, int) or 4 * t + p > 1:
                        pe.wait_ge(s_hb, 4 * t + p - 1)
                    for cc in range(2):
                        inner = (2 * p + cc) * P
                        for w in range(2):
                            for c in range(C2):
                                for lw, lx in ((0, 0), (0, 1), (1, 0)):
                                    last = pe.matmul(psT[:, p % 2, w, cc * TILE:(cc + 1) * TILE], w13[:, slot, w, lw, c, inner:inner + P],
                                                     mxt[:, slot, 2 * lx + c], start=(c == 0 and lw + lx == 0), stop=(c == 1 and lw == 1))
                    last.then_inc(s_h, 1)

                def second_products(t, slot):
                    pe.wait_ge(s_hl, 4 * t + 4)
                    pe.wait_ge(s_w2[slot], w2turn(t))
                    if not isinstance(t, int) or t > 1:
                        pe.wait_ge(s_ye, t - 1)
                    for h in range(C2):
                        for c in range(NI):
                            for lh, lw in ((0, 0), (0, 1), (1, 0)):
                                last = pe.matmul(psS[:, slot, h * D:(h + 1) * D], hhl[:, slot, lh, c, h * P:(h + 1) * P], w2[:, slot, lw, c],
                                                 start=(c == 0 and lh + lw == 0), stop=(c == NI - 1 and lh == 1))
                    last.then_inc(s_y, 1)

                wv, w2v = [None], [None]

                def wturn(t):
                    return 16 * (t // 2 + 1) if isinstance(t, int) else wv[0]

                def w2turn(t):
                    return 16 * (t // 2 + 1) if isinstance(t, int) else w2v[0]

                def tile(t, slot, weight=False, last=False):
                    first_products(t, slot, 0)
                    if not isinstance(t, int) or t > 0:
                        second_products(t - 1, 1 - slot)
                    first_products(t, slot, 1)
                    first_products(t, slot, 2)
                    if weight:
                        pe.wait_ge(s_fa, t + 1)
                        pe.matmul(psU[:, t:t + 1], ones32[:], fabs[:, t:t + 1], start=True, stop=True).then_inc(s_fr, 1)
                    if not last:
                        turned(t + 1, 1 - slot)
                    first_products(t, slot, 3)

                turned(0, 0)
                for t in range(3):
                    tile(t, t % 2, weight=True)
                with pe.Fori(0, (NT - 5) // 2) as j:
                    for r in range(2):
                        wv[0] = (j + (3 + r) // 2 + 1) * 16
                        w2v[0] = (j + 2) * 16
                        jv[0] = (j + 3) * 16
                        tile(j * 2 + (3 + r), (3 + r) % 2)
                tile(NT - 2, (NT - 2) % 2)
                tile(NT - 1, (NT - 1) % 2, last=True)
                second_products(NT - 1, (NT - 1) % 2)

        attention(1)

        with nc.Block() as block:
            at[0] = 0
            xf = part(4 * D).rearrange("p (s n) -> p s n", s=4)
            xnf = part(D)
            q1f = part(D)
            q1 = part(D // 2).bitcast(BF16)
            q1t = part(D).bitcast(BF16).rearrange("p (s n) -> p s n", s=2)
            sgf = part(1024).rearrange("p (s n) -> p s n", s=2)
            hbf = part(INNER)
            q2 = part(INNER).bitcast(BF16).rearrange("p (s n) -> p s n", s=2)
            q2t = part(INNER // 2).bitcast(BF16)
            of = part(2 * D).rearrange("p (s n) -> p s n", s=2)
            psM_b, psU_b = psM[:, :].bitcast(BF16), psU[:, :].bitcast(BF16)
            NU = TOK // P
            F1, F2 = 8, 4

            def tiles(body):
                def run(eng):
                    for u in range(2):
                        body(u, 0)
                    with eng.Fori(0, NU // 4 - 1) as j:
                        for r in range(4):
                            body(2 + r, j)
                    for u in range(NU - 2, NU):
                        body(u, 0)
                return run

            def num(s, j, off=0):
                return s + off if isinstance(j, int) else j * 4 + (s + off)

            def halves(s, j, off=0):
                return (s + off) // 2 if isinstance(j, int) else j * 2 + (s + off) // 2

            def quarters(s, j, off=0):
                return (s + off) // 4 if isinstance(j, int) else j + (s + off) // 4

            def static(j):
                return isinstance(j, int)

            @block.sync
            def _(sp):
                def load(s, j, off):
                    sp.dma_start(xf[:, (s + off) % 4], x3_d[bass.ds(num(s, j, off) * P, P)]).then_inc(s_xf[(s + off) % 4], 16)

                def body(s, j):
                    if not static(j) or s + 2 < NU:
                        if not static(j) or s > 1:
                            sp.wait_ge(s_res, num(s, j, -1))
                        load(s, j, 2)
                    if not static(j) or s > 0:
                        sp.wait_ge(s_res, num(s, j))
                        sp.dma_start(out[bass.ds(num(s, j, -1) * P, P)], of[:, (s + 1) % 2]).then_inc(s_ost[(s + 1) % 2], 16)

                load(0, 0, 0)
                load(1, 0, 0)
                tiles(body)(sp)
                sp.wait_ge(s_res, NU)
                sp.dma_start(out[(NU - 1) * P:NU * P], of[:, 1]).then_inc(s_ost[1], 16)
                for k in range(2):
                    sp.wait_ge(s_ost[k], 16 * (NU // 2))

            @block.gpsimd
            def _(pool):
                def body(s, j, off=1):
                    if static(j) and s + off >= NU:
                        return
                    pool.wait_ge(s_f1, F1 * num(s, j, off) + 2)
                    apart(pool)
                    pool.tensor_scalar(frs[:, 0:1], fmv[:, 1:2], EPS, None, ALU.add).then_inc(s_fv, 1)
                    pool.wait_ge(s_fv, num(s, j, off) + 1)
                    pool.tensor_tensor(frs[:, 1:2], frs[:, 0:1], mhalf[:, 0:1], ALU.pow).then_inc(s_frs, 1)

                body(0, 0, 0)
                tiles(body)(pool)

            @block.scalar
            def _(act):
                def body(s, j):
                    u = num(s, j)
                    for hf in range(2):
                        act.wait_ge(s_gu, 2 * u + hf + 1)
                        if not static(j) or s > 0:
                            act.wait_ge(s_hm, 2 * u + hf - 1)
                        act.activation(sgf[:, hf], psT[:, hf, 0], ACT.Silu, scale=fsc[:, s % 2, 0:1]).then_inc(s_sil, 1)
                    if not static(j) or s > 0:
                        turned(num(s, j, -1))
                    act.wait_ge(s_f2, F2 * u + 4)
                    act.activation(hbf[:], hbf[:], ACT.Identity, bias=rnd[:, 0:1], scale=sc2[:, 0:1]).then_inc(s_q2a, 1)

                def turned(v):
                    act.wait_ge(s_q2p, v + 1)
                    act.activation(q2t[:], psU_b, ACT.Copy).then_inc(s_q2t, 1)

                tiles(body)(act)
                turned(NU - 1)

            @block.vector
            def _(dve):
                def front(s, j, off, half):
                    v = num(s, j, off)

                    def step(k, ins):
                        ins.then_inc(s_f1, 1)
                        dve.wait_ge(s_f1, F1 * v + k)
                        if k == 1:
                            apart(dve)
                    x = xf[:, (s + off) % 4]
                    if half == 0:
                        dve.wait_ge(s_xf[(s + off) % 4], 16 * quarters(s, j, off) + 16)
                        step(1, dve.bn_stats(fst6[:], x))
                        step(2, dve.bn_aggr(fmv[:], fst6[:]))
                        return
                    dve.wait_ge(s_frs, v + 1)
                    step(3, dve.tensor_scalar(xnf[:], x, fmv[:, 0:1], frs[:, 1:2], ALU.subtract, ALU.mult))
                    step(4, dve.tensor_reduce(am[:, 0:1], xnf[:], X, ALU.max, apply_absolute_value=True))
                    step(5, dve.tensor_scalar(am[:, 0:1], am[:, 0:1], EPS, None, ALU.max))
                    dve.tensor_scalar(fsc[:, (s + off) % 2], fdeq[:, 0:2], am[:, 0:1], None, ALU.mult)
                    step(6, dve.reciprocal(am[:, 1:2], am[:, 0:1]))
                    step(7, dve.tensor_scalar(am[:, 1:2], am[:, 1:2], 127.0, None, ALU.mult))
                    step(8, dve.tensor_scalar(q1f[:], xnf[:], am[:, 1:2], RND, ALU.mult, ALU.add))
                    dve.tensor_scalar(q1[:], q1f[:], RND, None, ALU.subtract).then_inc(s_q1, 1)

                def q1_turned(v, slot):
                    dve.wait_ge(s_q1p, v + 1)
                    dve.tensor_copy(q1t[:, slot], psM_b[:, 0:D]).then_inc(s_q1t, 1)

                def residual(s, j, off):
                    v = num(s, j, off)
                    dve.wait_ge(s_dn, v + 1)
                    if not static(j) or s + off > 1:
                        dve.wait_ge(s_ost[(s + off) % 2], 16 * halves(s, j, off))
                    dve.scalar_tensor_tensor(out=of[:, (s + off) % 2], in0=psS[:, (s + off) % 2, 0:D], scalar=fd[:, (s + off) % 2:(s + off) % 2 + 1],
                                             in1=xf[:, (s + off) % 4], op0=ALU.mult, op1=ALU.add).then_inc(s_res, 1)

                def body(s, j):
                    u = num(s, j)
                    more = not static(j) or s + 1 < NU
                    if more:
                        front(s, j, 1, 0)
                    for hf in range(2):
                        dve.wait_ge(s_sil, 2 * u + hf + 1)
                        dve.scalar_tensor_tensor(out=hbf[:, hf * 512:(hf + 1) * 512], in0=psT[:, hf, 1], scalar=fsc[:, s % 2, 1:2], in1=sgf[:, hf],
                                                 op0=ALU.mult, op1=ALU.mult).then_inc(s_hm, 1)
                    dve.wait_ge(s_hm, 2 * u + 2)

                    def step(k, ins):
                        ins.then_inc(s_f2, 1)
                        dve.wait_ge(s_f2, F2 * u + k)
                    step(1, dve.tensor_reduce(am[:, 2:3], hbf[:], X, ALU.max, apply_absolute_value=True))
                    step(2, dve.tensor_scalar(am[:, 2:3], am[:, 2:3], EPS, None, ALU.max))
                    dve.tensor_scalar(fd[:, s % 2:s % 2 + 1], am[:, 2:3], fdeq[:, 2:3], tg[:, 3:4], ALU.mult, ALU.mult)
                    step(3, dve.reciprocal(am[:, 3:4], am[:, 2:3]))
                    step(4, dve.tensor_scalar(sc2[:], am[:, 3:4], 127.0, None, ALU.mult))
                    if more:
                        front(s, j, 1, 1)
                    dve.wait_ge(s_q2a, u + 1)
                    dve.tensor_scalar(q2[:, s % 2], hbf[:], RND, None, ALU.subtract).then_inc(s_q2, 1)
                    if not static(j) or s > 0:
                        residual(s, j, -1)
                    if more:
                        q1_turned(num(s, j, 1), (s + 1) % 2)

                dve.memset(rnd[:], RND)
                front(0, 0, 0, 0)
                front(0, 0, 0, 1)
                q1_turned(0, 0)
                tiles(body)(dve)
                residual(NU - 1, 0, 0)

            @block.tensor
            def _(pe):
                def turn1(s, j, off):
                    pe.wait_ge(s_q1, num(s, j, off) + 1)
                    if not static(j) or s + off > 0:
                        pe.wait_ge(s_q1t, num(s, j, off))
                    for c in range(C2):
                        last = pe.transpose(psM_b[:, c * P:(c + 1) * P], q1[:, c * P:(c + 1) * P], idb[:])
                    last.then_inc(s_q1p, 1)

                def down(s, j, off):
                    v = num(s, j, off)
                    pe.wait_ge(s_q2, v + 1)
                    if not static(j) or s + off > 0:
                        pe.wait_ge(s_q2t, v)
                    for c in range(NI):
                        last = pe.transpose(psU_b[:, c * P:(c + 1) * P], q2[:, (s + off) % 2, c * P:(c + 1) * P], idb[:])
                    last.then_inc(s_q2p, 1)
                    pe.wait_ge(s_q2t, v + 1)
                    if not static(j) or s + off > 1:
                        pe.wait_ge(s_res, num(s, j, off - 1))
                    for c in range(NI):
                        last = pe.matmul(psS[:, (s + off) % 2, 0:D], q2t[:, c * P:(c + 1) * P], fwt[:, 2, c * D:(c + 1) * D], start=(c == 0), stop=(c == NI - 1))
                    last.then_inc(s_dn, 1)

                def body(s, j):
                    u = num(s, j)
                    pe.wait_ge(s_q1t, u + 1)
                    for hf in range(2):
                        if not static(j) or s > 0:
                            pe.wait_ge(s_hm, 2 * u + hf - 1)
                        for w in range(2):
                            for c in range(C2):
                                last = pe.matmul(psT[:, hf, w], q1t[:, s % 2, c * P:(c + 1) * P], fwt[:, w, c * INNER + hf * 512:c * INNER + hf * 512 + 512],
                                                 start=(c == 0), stop=(c == C2 - 1))
                        last.then_inc(s_gu, 1)
                    if not static(j) or s > 0:
                        down(s, j, -1)
                    if not static(j) or s + 1 < NU:
                        turn1(s, j, 1)

                turn1(0, 0, 0)
                tiles(body)(pe)
                down(NU - 1, 0, 0)


_OUTS = [((B, S, D), "float32")]


def lay_out(v):
    v = {k: np.asarray(x) for k, x in v.items()}
    cols = np.array([[(2 * (2 * hq + g) + par) * HD + d for par in range(2) for d in range(HD) for hq in range(4)] for g in range(C2)]).ravel()

    def chunks(w):
        return w.reshape(-1, P, w.shape[-1]).transpose(1, 0, 2)

    def attn(q, k, vw, o):
        return np.stack([chunks(v[q].T[:, cols]), chunks(v[k].T[:, cols]), chunks(v[vw].T), chunks(v[o].T)], 1).reshape(P, -1)

    moe = np.stack([np.stack([chunks(v["L0_ffn_w1"][e].T).reshape(P, -1), chunks(v["L0_ffn_w3"][e].T).reshape(P, -1),
                              chunks(v["L0_ffn_w2"][e].T).reshape(P, -1)]) for e in range(E)]).reshape(3 * E, P, 2048)
    return {
        "x": v["x"].reshape(TOK, D),
        "ctx": v["ctx_1024"].transpose(0, 2, 1).reshape(B, C2, P, S).transpose(0, 2, 1, 3),
        "g": np.broadcast_to(np.stack([v["g_xattn"], v["g_ffn"]], 1).reshape(1, 4), (P, 4)),
        "gate": chunks(v["L0_ffn_gate_w"].T),
        "mask": chunks(v["mask_SxS2_ff0"]),
        "kpm": v["mask_BxS2_bf0"].view(np.int32),
        "bqk": np.stack([v[b][cols].reshape(C2, P).T for b in ("L1_xattn_b_q", "L1_xattn_b_k")], 1),
        "bv": np.broadcast_to(v["L1_xattn_b_v"], (P, D)),
        "bo": np.broadcast_to(v["L1_xattn_b_o"], (P, D)),
        "aw": np.stack([attn("L0_xattn_Wq", "L0_xattn_Wk", "L0_xattn_Wv", "L0_xattn_Wo"),
                        attn("L1_xattn_w_q", "L1_xattn_w_k", "L1_xattn_w_v", "L1_xattn_w_o")]),
        "moe": moe,
        "fw": np.stack([chunks(v["L1_ffn_w_gate"].T).reshape(P, -1), chunks(v["L1_ffn_w_up"].T).reshape(P, -1),
                        chunks(v["L1_ffn_w_down"].T).reshape(P, -1)]),
    }


def kernel(**inputs):
    import concourse.bacc as bacc
    from concourse.bass_utils import run_bass_kernel_spmd

    nc = bacc.Bacc("TRN2", target_bir_lowering=False, num_devices=1)
    arrays, aps = {}, {}
    for name, x in lay_out(inputs).items():
        arrays[f"in_{name}"] = np.ascontiguousarray(x)
        aps[name] = nc.dram_tensor(f"in_{name}", x.shape, mybir.dt.from_np(x.dtype), kind="ExternalInput").ap()
    out = nc.dram_tensor("out_0", (TOK, D), F32, kind="ExternalOutput").ap()
    build(nc, aps, out)
    r = run_bass_kernel_spmd(nc, [arrays], core_ids=[0])
    return r.results[0]["out_0"].reshape(B, S, D)
```

```python
from contextlib import ExitStack

import numpy as np

import concourse.bass as bass
from concourse import mybir

F32, F16, BF16 = mybir.dt.float32, mybir.dt.float16, mybir.dt.bfloat16
I32, U32, U8 = mybir.dt.int32, mybir.dt.uint32, mybir.dt.uint8
ACT = mybir.ActivationFunctionType
ALU = mybir.AluOpType
X = mybir.AxisListType.X

P = 128
B, S, D = 16, 256, 256
TOK = B * S
H, HD = 16, 16
PAIRS = H // 2
C2 = D // P
E, INNER = 8, 1024
NI = INNER // P
WSC = 64.0
LOGIT = 1.0 / (WSC * WSC * 4.0)
SHIFT = 256.0
MASKED = -30000.0
TILE = 256
REGION = TOK + TILE
NT = (2 * TOK + E * (TILE - 1)) // TILE
KPM, SHA = 96, 97
STACK = 99
RND = 12582912.0
EPS = 1e-5


class Misc:
    SECOND = ("M1", "XT", "K", "Q", "V", "M0", "RK")

    def __init__(self, layer, base):
        if layer == 0:
            self.steps = {0: "K", 1: "GT", 2: "M1", 3: "GS", 4: "XT", 5: "UT0",
                          6: "Q", 7: "UT1", 8: "M0", 9: "OT", 10: "V", 11: "WO", 12: "RK"}
        else:
            self.steps = {0: "M1", 2: "XT", 3: "UT0", 4: "K", 6: "UT1",
                          7: "Q", 9: "OT", 10: "M0", 11: "V", 14: "WO"}
        self.at = {name: s for s, name in self.steps.items()}
        self.lag = {"M1": 1, "XT": -1, "UT0": 2, "Q": -1, "UT1": 2, "K": -1, "OT": 2, "V": -1, "M0": 0, "WO": 2,
                    "RK": 3, "GT": 3, "GS": 3}
        self.order = [self.steps[s] for s in sorted(self.steps)]
        self.start, n = {}, base
        for i in range(-1, B + 4):
            self.start[i] = n
            n += sum(self.has(i, name) for name in self.order)
        self.end = n
        self.first_full = 4
        self.last_full = B - 4

    def has(self, i, name):
        return 0 <= i - self.lag[name] < B

    def before(self, i, name):
        at = self.order.index(name)
        if isinstance(i, int):
            return self.start[i] + sum(self.has(i, x) for x in self.order[:at])
        return i * len(self.order) + (self.start[self.first_full] - self.first_full * len(self.order) + at)

    def previous(self, i, name):
        at = self.order.index(name)
        back = [(i, x) for x in reversed(self.order[:at])] + [(i - 1, x) for x in reversed(self.order)]
        back = [(k, x) for k, x in back if (x in self.SECOND) == (name in self.SECOND)]
        if not isinstance(i, int):
            return back[0]
        return next(((k, x) for k, x in back if self.has(k, x)), None)


def build(nc, a, out):
    ctx = ExitStack()
    with ctx:
        def sb(name, shape, dt):
            return ctx.enter_context(nc.sbuf_tensor(name, shape, dt))

        def pb(name, shape, dt):
            return ctx.enter_context(nc.psum_tensor(name, shape, dt))

        def sem(name):
            return ctx.enter_context(nc.semaphore(name))

        def dram(name, shape, dt):
            return nc.dram_tensor(name, shape, dt).ap()

        x1_d = dram("x1_d", [TOK, D], F32)
        x2_d = dram("x2_d", [TOK, D], F32)
        x3_d = dram("x3_d", [TOK, D], F32)
        routed_d = dram("routed_d", [E * REGION, 2 * D], F16)
        y_d = dram("y_d", [NT * TILE, D], F32)
        ws_d = dram("ws_d", [3 * E, P, 4096], F16)
        kpm_d = dram("kpm_d", [2 * B, S], F16)

        psS = pb("psS", [P, 2, 512], F32)
        psT = pb("psT", [P, 2, 2, 512], F32)
        psU = pb("psU", [P, 512], F32)
        psM = pb("psM", [P, 512], F32)
        psM16 = psM[:, :].bitcast(F16)
        psH = psT[:, :, :, :].rearrange("p a b n -> p (a b) n")
        psN = psH[:, 3]

        id32 = sb("id32", [P, P], F32)
        id16 = sb("id16", [P, P], F16)
        idb = sb("idb", [P, P], BF16)
        idmask = sb("idmask", [P, P], F16)
        lower = sb("lower", [P, P], F16)
        ones16 = sb("ones16", [P, P], F16)
        aw = sb("aw", [P, 2, 2, 4, C2, D], F16)
        bqk = sb("bqk", [P, 2, C2], F32)
        bv = sb("bv", [P, D], F32)
        bo = sb("bo", [P, D], F32)
        zero = sb("zero", [P, D], F32)
        zero16 = sb("zero16", [P, 2, 2 * D], F16)
        gts = sb("gts", [P, 4], F32)
        tg = sb("tg", [P, 4], F32)
        tg64 = sb("tg64", [P, 4], F32)
        gate = sb("gate", [P, C2, E], F32)
        gatehl = sb("gatehl", [P, 2, C2, E], F16)
        maskf = sb("maskf", [P, C2, S], F32)
        maskh = sb("maskh", [P, C2, S], F16)
        maskThl = sb("maskThl", [P, 2, C2, S], F16)
        maxmask = sb("maxmask", [P, C2], F32)
        kpm8 = sb("kpm8", [B, S], U8)
        kpmh = sb("kpmh", [B, S], F16)
        kconst = sb("kconst", [2, 2, PAIRS * S], F16)
        qs = sb("qs", [P, 3, PAIRS, S], F16)
        ks = sb("ks", [P, 3, 2, PAIRS, S], F16)
        vv = sb("vv", [P, 3, C2, H, 32], F32)
        mx = sb("mx", [P, 2, C2, 8], F32)
        mt = sb("mt", [8, 2, S], F16)
        lnst = sb("lnst", [P, C2, 6], F32)
        lnmv = sb("lnmv", [P, C2, 2], F32)
        lnrs = sb("lnrs", [P, 2, C2], F32)
        l2st = sb("l2st", [P, C2, 6], F32)
        l2mv = sb("l2mv", [P, C2, 2], F32)
        l2rs = sb("l2rs", [P, 2, C2], F32)
        mhalf = sb("mhalf", [P, C2], F32)
        rden = sb("rden", [P, C2, H], F32)
        w8 = sb("w8", [P, E], F32)
        sc = sb("sc", [P, 2, C2, E], F32)
        eqm = sb("eqm", [P, C2, E], F32)
        top = sb("top", [P, 2, C2], F32)
        wmax = sb("wmax", [P, C2], F32)
        oh = sb("oh", [P, 2, C2, E], F32)
        chosen = sb("chosen", [P, C2, E], F16)
        runb = sb("runb", [P, E], F32)
        rank = sb("rank", [P, C2, E], F32)
        prod = sb("prod", [P, 2, C2, E], F32)
        row = sb("row", [P, 2, C2], F32)
        rowi = sb("rowi", [P, 2, C2], U32)
        OH = sb("OH", [P, B, 2 * C2 * E], F32)
        ROW = sb("ROW", [P, B, 2 * C2], F32)
        TOP = sb("TOP", [P, B, 2 * C2], F32)
        WAB = sb("WAB", [P, 2, B * C2], F32)
        POS = sb("POS", [P, B, 2 * C2], U32)
        gidx = sb("gidx", [P, 4], U32)
        cnt = sb("cnt", [P, E], F32)
        ntile = sb("ntile", [P, E], F32)
        cum = sb("cum", [P, E + 1], F32)
        base = sb("base", [P, E], F32)
        delta = sb("delta", [P, E], F32)
        dbase = sb("dbase", [P, E - 1], F32)
        lim = sb("lim", [P, 1], F32)
        tt = sb("tt", [P, NT], F32)
        ge = sb("ge", [P, NT, E - 1], F32)
        gd = sb("gd", [P, NT, E - 1], F32)
        gs = sb("gs", [P, NT], F32)
        scan = sb("scan", [P, 2, E], F32)
        eid = sb("eid", [P, NT], F32)
        rowf = sb("rowf", [P, NT], F32)
        rowt = sb("rowt", [P, NT], I32)
        eidt = sb("eidt", [P, NT], I32)
        endi = sb("endi", [P, E], I32)
        posf = sb("posf", [P, 4 * B], F32)
        tdif = sb("tdif", [P, B * C2], F32)
        tsum = sb("tsum", [P, B * C2], F32)
        fst = sb("fst", [P, 2048], F32)
        fwt = sb("fwt", [P, 3, 2048], BF16)
        fabs = sb("fabs", [P, 3], F32)
        ones32 = sb("ones32", [P, P], F32)
        fmean = sb("fmean", [P, 3], F32)
        fscale = sb("fscale", [P, 3], F32)
        fst6 = sb("fst6", [P, 6], F32)
        fmv = sb("fmv", [P, 2], F32)
        frs = sb("frs", [P, 2], F32)
        am = sb("am", [P, 4], F32)
        fsc = sb("fsc", [P, 2, 2], F32)
        fd = sb("fd", [P, 2], F32)
        rnd = sb("rnd", [P, 1], F32)
        big = sb("big", [P, 2, 3, 2, 2048], F16)
        bigf = big[:, :, :, :, :].rearrange("p a b c n -> p (a b c n)").bitcast(F32)
        pt = bigf[:, 0:4096].rearrange("p (s h n) -> p s h n", s=4, h=2)
        wst = bigf[:, 4096:8192].rearrange("p (s n) -> p s n", s=2)
        wsp = bigf[:, 8192:12288].bitcast(F16).rearrange("p (s l n) -> p s l n", s=2, l=2)
        work = sb("work", [P, 10752], F32)
        at = [0]

        def part(words):
            at[0] += words
            assert at[0] <= 10752
            return work[:, at[0] - words:at[0]]

        xin = part(1536).rearrange("p (s c d) -> p s c d", s=3, c=C2)
        cin = part(1536).rearrange("p (s c d) -> p s c d", s=3, c=C2)
        xn = part(512).rearrange("p (c d) -> p c d", c=C2)
        xhl = part(512).bitcast(F16).rearrange("p (l c n) -> p l c n", l=2, c=C2)
        qhl = part(512).bitcast(F16).rearrange("p (l n) -> p l n", l=2)
        khl = part(512).bitcast(F16).rearrange("p (l n) -> p l n", l=2)
        chl = part(512).bitcast(F16).rearrange("p (l c n) -> p l c n", l=2, c=C2)
        uu = part(1024).rearrange("p (s n) -> p s n", s=2)
        oo = part(512).rearrange("p (c d) -> p c d", c=C2)
        ohl = part(512).bitcast(F16).rearrange("p (l c n) -> p l c n", l=2, c=C2)
        xo = part(512).rearrange("p (c d) -> p c d", c=C2)
        xn1 = part(512).rearrange("p (c d) -> p c d", c=C2)
        xg = part(512).bitcast(F16).rearrange("p (k n) -> p k n", k=4)
        xr_ga = part(1536)
        xr = xr_ga.bitcast(F16).rearrange("p (s c n) -> p s c n", s=3, c=C2)
        ga = xr_ga[:, 0:1024].rearrange("p (k c d) -> p k c d", k=2, c=C2)
        at[0] = 0
        mxr = part(1024).bitcast(F16).rearrange("p (s c n) -> p s c n", s=2, c=C2)
        mxt = part(1024).bitcast(F16).rearrange("p (s k n) -> p s k n", s=2, k=4)
        sg = part(1024).rearrange("p (s n) -> p s n", s=2)
        hb = part(1024).rearrange("p (s n) -> p s n", s=2)
        hhl = part(4096).bitcast(F16).rearrange("p (s l c n) -> p s l c n", s=2, l=2, c=NI)
        ye = part(1024).rearrange("p (s n) -> p s n", s=2)

        s_id = sem("s_id")
        s_const = sem("s_const")
        s_set = sem("s_set")
        s_setw = sem("s_setw")
        s_wh = sem("s_wh")
        s_dset = sem("s_dset")
        s_tg = sem("s_tg")
        s_kpm = sem("s_kpm")
        s_zero = sem("s_zero")
        s_krow = sem("s_krow")
        s_maskt = sem("s_maskt")
        s_apart = sem("s_apart")

        def apart(eng):
            eng.sem_inc(s_apart, 1)

        s_x = [sem(f"s_xin{k}") for k in range(3)]
        s_c = [sem(f"s_cin{k}") for k in range(3)]
        s_ln = sem("s_ln")
        s_var = sem("s_var")
        s_rs = sem("s_rs")
        s_xn = sem("s_xn")
        s_xh = sem("s_xh")
        s_xl = sem("s_xl")
        s_ch = sem("s_ch")
        s_cl = sem("s_cl")
        s_qh = sem("s_qh")
        s_ql = sem("s_ql")
        s_kh = sem("s_kh")
        s_kl = sem("s_kl")
        s_v = sem("s_v")
        s_qst = sem("s_qst")
        s_kst = sem("s_kst")
        s_s = sem("s_s")
        s_mx = sem("s_mx")
        s_mt = sem("s_mt")
        s_sh = sem("s_sh")
        s_t = sem("s_t")
        s_exp = sem("s_exp")
        s_pv = sem("s_pv")
        s_u = sem("s_u")
        s_rd = sem("s_rd")
        s_o = sem("s_o")
        s_oh = sem("s_oh")
        s_ol = sem("s_ol")
        s_xo = sem("s_xo")
        s_bo = sem("s_bo")
        s_x1 = sem("s_x1")
        s_xst = sem("s_xst")
        s_md = sem("s_md")
        s_l2 = sem("s_l2")
        s_var2 = sem("s_var2")
        s_rs2 = sem("s_rs2")
        s_xn1 = sem("s_xn1")
        s_xrh = sem("s_xrh")
        s_xrl = sem("s_xrl")
        s_xg = sem("s_xg")
        s_rt = sem("s_rt")
        s_scat = sem("s_scat")
        s_wld = [sem(f"s_wld{k}") for k in range(2)]
        s_wsh = sem("s_wsh")
        s_wsl = sem("s_wsl")
        s_wss = sem("s_wss")
        s_wst = [sem(f"s_wst{k}") for k in range(2)]
        s_ga = sem("s_ga")
        s_gi = sem("s_gi")
        s_mix = sem("s_mix")
        s_x2 = sem("s_x2")

        s_end = sem("s_end")
        s_tab = sem("s_tab")
        s_tt = sem("s_tt")
        s_zf = sem("s_zf")
        s_rf = sem("s_rf")
        s_te = sem("s_te")
        s_mr = [sem(f"s_mr{k}") for k in range(2)]
        s_w13 = [sem(f"s_w13_{k}") for k in range(2)]
        s_w2 = [sem(f"s_w2_{k}") for k in range(2)]
        s_yst = [sem(f"s_yst{k}") for k in range(2)]
        s_xtp = sem("s_xtp")
        s_xt = sem("s_xt")
        s_h = sem("s_h")
        s_sg = sem("s_sg")
        s_hb = sem("s_hb")
        s_hh = sem("s_hh")
        s_hl = sem("s_hl")
        s_y = sem("s_y")
        s_ye = sem("s_ye")
        s_fw = sem("s_fw")
        s_fa = sem("s_fa")
        s_fr = sem("s_fr")
        s_ft = sem("s_ft")
        s_fq = sem("s_fq")
        s_xf = [sem(f"s_xf{k}") for k in range(4)]
        s_ost = [sem(f"s_ost{k}") for k in range(2)]
        s_f1 = sem("s_f1")
        s_f2 = sem("s_f2")
        s_fv = sem("s_fv")
        s_st = sem("s_st")
        s_xnf = sem("s_xnf")
        s_xs = [sem(f"s_xs{k}") for k in range(2)]
        s_frs = sem("s_frs")
        s_q1 = sem("s_q1")
        s_q1p = sem("s_q1p")
        s_q1t = sem("s_q1t")
        s_gu = sem("s_gu")
        s_sil = sem("s_sil")
        s_hm = sem("s_hm")
        s_q2a = sem("s_q2a")
        s_q2 = sem("s_q2")
        s_q2p = sem("s_q2p")
        s_q2t = sem("s_q2t")
        s_dn = sem("s_dn")
        s_res = sem("s_res")
        RF_TDIF = 4 + 1 + 3 + 4 + 2 + 1 + 4 + 1 + 2 + 1

        RT = 18
        xh, xl = xhl[:, 0], xhl[:, 1]

        with nc.Block() as block:
            wld = bigf[:, 0:4096].rearrange("p (l n) -> p l n", l=2)

            @block.sync
            def _(sp):
                for dst, src in ((gts[:], a["g"]), (gate[:], a["gate"]), (maskf[:], a["mask"]), (kpm8[:].bitcast(I32), a["kpm"]),
                                 (bqk[:], a["bqk"]), (bv[:], a["bv"]), (bo[:], a["bo"])):
                    sp.dma_start(dst, src).then_inc(s_set, 16)
                for l in range(2):
                    sp.dma_start(wld[:, l, :], a["aw"][l]).then_inc(s_setw, 16)
                sp.wait_ge(s_const, 1)
                sp.wait_ge(s_kpm, 1)
                sp.dma_start(kpm_d[0:B, :], kpmh[:]).then_inc(s_krow, 16)
                sp.dma_start(kpm_d[B:2 * B, :], zero16[0:B, 0, 0:S]).then_inc(s_krow, 16)
                sp.wait_ge(s_zero, 1)
                for slot in range(3):
                    for ab in range(2):
                        sp.dma_start(ks[SHA:SHA + 2, slot, ab].rearrange("p a t -> p (a t)"), kconst[:, ab]).then_inc(s_krow, 16)
                sp.wait_ge(s_krow, 16 * 8)

            @block.gpsimd
            def _(pool):
                pool.memset(id32[:], 0.0)
                pool.memset(id16[:], 0.0)
                pool.memset(idb[:], 0.0)
                pool.memset(idmask[:], 0.0)
                pool.memset(lower[:], 0.0)
                pool.memset(ones16[:], 1.0)
                pool.memset(ones32[:], 1.0)
                pool.memset(kconst[:], 0.0).then_inc(s_id, 1)
                pool.wait_ge(s_id, 1)
                for t, v in ((id32, 1.0), (id16, 1.0), (idb, 1.0), (idmask, 1.0 / LOGIT)):
                    pool.affine_select(out=t[:], in_=t[:], compare_op=ALU.not_equal, fill=v, base=0,
                                       pattern=[[-1, P]], channel_multiplier=1)
                pool.affine_select(out=lower[:], in_=lower[:], compare_op=ALU.is_ge, fill=1.0, base=0,
                                   pattern=[[-1, P]], channel_multiplier=1)
                pool.affine_select(out=kconst[:], in_=kconst[:], compare_op=ALU.not_equal, fill=SHIFT, base=0,
                                   pattern=[[-1, 2], [0, PAIRS * S]], channel_multiplier=1)
                pool.iota(w8[:], [[-1, E]], base=E, channel_multiplier=0, allow_small_or_imprecise_dtypes=True)
                pool.iota(runb[:], [[REGION, E]], base=0, channel_multiplier=0, allow_small_or_imprecise_dtypes=True)
                pool.memset(mhalf[:], -0.5)
                pool.memset(zero[:], 0.0)
                pool.memset(zero16[:], 0.0).then_inc(s_const, 1)
                pool.memset(vv[:, :, :, :, HD + 1:32], 0.0)
                pool.memset(vv[:, :, :, :, HD:HD + 1], 1.0).then_inc(s_const, 1)
                pool.wait_ge(s_const, 2)
                pool.memset(qs[KPM:KPM + 1, :, :, :], 1.0 / LOGIT)

            @block.scalar
            def _(act):
                act.wait_ge(s_set, 7 * 16)
                act.activation(tg[:], gts[:], ACT.Tanh).then_inc(s_tg, 1)
                act.wait_ge(s_tg, 1)
                act.activation(tg64[:], tg[:], ACT.Copy, scale=1.0 / WSC)
                act.activation(gatehl[:, 0], gate[:], ACT.Copy, scale=WSC).then_inc(s_wh, 1)
                for l in range(2):
                    act.wait_ge(s_setw, 32)
                    act.activation(aw[:, l, 0].rearrange("p w c n -> p (w c n)"), wld[:, l, :], ACT.Copy, scale=WSC).then_inc(s_wh, 1)

            @block.vector
            def _(dve):
                dve.memset(ks[:, :, :, :, :], 0.0).then_inc(s_zero, 1)
                dve.wait_ge(s_set, 7 * 16)
                dve.tensor_reduce(maxmask[:], maskf[:], X, ALU.max).then_inc(s_dset, 1)
                dve.wait_ge(s_dset, 1)
                for c in range(C2):
                    dve.tensor_scalar(maskf[:, c], maskf[:, c], maxmask[:, c:c + 1], MASKED, ALU.subtract, ALU.max).then_inc(s_dset, 1)
                dve.wait_ge(s_dset, 3)
                dve.tensor_copy(maskh[:], maskf[:]).then_inc(s_dset, 1)
                dve.tensor_scalar(kpmh[:], kpm8[:], MASKED, None, ALU.mult).then_inc(s_kpm, 1)
                dve.tensor_scalar(bqk[:], bqk[:], WSC, None, ALU.mult)
                dve.wait_ge(s_tg, 1)
                dve.tensor_scalar(bo[:], bo[:], tg[:, 2:3], None, ALU.mult)
                dve.wait_ge(s_wh, 1)
                dve.scalar_tensor_tensor(out=gatehl[:, 1], in0=gate[:], scalar=WSC, in1=gatehl[:, 0], op0=ALU.mult, op1=ALU.subtract)
                for l in range(2):
                    dve.wait_ge(s_wh, l + 2)
                    dve.scalar_tensor_tensor(out=aw[:, l, 1].rearrange("p w c n -> p (w c n)"), in0=wld[:, l, :], scalar=WSC,
                                             in1=aw[:, l, 0].rearrange("p w c n -> p (w c n)"), op0=ALU.mult, op1=ALU.subtract)
                dve.wait_ge(s_maskt, 1)
                dve.tensor_copy(maskThl[:, 0], psM[:, :].rearrange("p (c n) -> p c n", c=C2)).then_inc(s_dset, 1)
                dve.wait_ge(s_dset, 5)
                dve.tensor_tensor(maskThl[:, 1], psM[:, :].rearrange("p (c n) -> p c n", c=C2), maskThl[:, 0], ALU.subtract)

            @block.tensor
            def _(pe):
                pe.wait_ge(s_const, 1)
                pe.wait_ge(s_dset, 3)
                for kc in range(C2):
                    for qc in range(C2):
                        last = pe.transpose(psM[:, kc * S + qc * P:kc * S + (qc + 1) * P], maskf[:, qc, kc * P:(kc + 1) * P], id32[:])
                last.then_inc(s_maskt, 1)

        def attention(L):
            misc = Misc(L, 0 if L == 0 else Misc(0, 0).end)
            xsrc, xres, xdst = (a["x"], a["x"], x1_d) if L == 0 else (x1_d, x2_d, x3_d)
            FULL = (misc.first_full, misc.last_full)
            LAST = B + 3 if L == 0 else B + 2

            def batch_rows(d, b):
                return d[bass.ds(b * S, S)].rearrange("(c p) d -> p c d", p=P)

            def valid(i, lag):
                return not isinstance(i, int) or 0 <= i - lag < B

            def iterations(eng, body):
                for i in range(-2, FULL[0]):
                    body(i, i % 3, i // 3)
                with eng.Fori(0, (FULL[1] - FULL[0] + 1) // 3) as j:
                    for k in range(FULL[0], FULL[0] + 3):
                        body(j * 3 + k, k % 3, j + k // 3)
                for i in range(FULL[1] + 1, LAST):
                    body(i, i % 3, i // 3)

            def landed(r, q):
                slot, turn = (r + 2) % 3, (r + 2) // 3
                before = L * len(range(slot, B, 3))
                return q * 16 + 16 * (turn + before + 1)

            def splits(i, lag=0):
                return L == 0 and (not isinstance(i, int) or 2 <= i - lag < 2 + 3 * E // 2)

            at = misc.at

            def bank(name):
                return psN if name in Misc.SECOND else psM[:, :]

            def head_slot(r, s):
                return (r + 2 + s) % 3

            SPLIT_STEPS = (3, 5, 7, 8, 11, 12, 13, 14)

            def piece(d, m):
                return d[bass.ds(m, 1)].rearrange("o p n -> (o p) n")

            def n(i, lag=0):
                return i + (L * B - lag)

            with nc.Block() as block:

                @block.sync
                def _(sp):
                    def load(i, slot):
                        if valid(i, 3):
                            sp.wait_ge(s_xn, 2 * n(i, 3) + 2)
                            apart(sp)
                            sp.wait_ge(s_cl, n(i, 3) + 1)
                            sp.wait_ge(s_ch, n(i, 3) + 1)
                        sp.dma_start(xin[:, slot], batch_rows(xsrc, i)).then_inc(s_x[slot], 16)
                        sp.dma_start(cin[:, slot], a["ctx"][bass.ds(i, 1)].rearrange("o p c n -> (o p) c n")).then_inc(s_c[slot], 16)

                    def shift(b, slot, half):
                        sp.wait_ge(s_mt, 2 * n(b) + 1 + half)
                        sp.dma_start(qs[SHA:SHA + 2, slot, 4 * half:4 * half + 4].rearrange("p a t -> p (a t)"), mt[:, half]).then_inc(s_sh, 16)

                    def store_weight(i, k):
                        m = (i - 2) * 2 + k
                        sp.wait_ge(s_wsl, m + 1)
                        apart(sp)
                        sp.dma_start(piece(ws_d, m), wsp[:, k].rearrange("p l n -> p (l n)")).then_inc(s_wst[k], 16)
                        if not isinstance(i, int) or m + 2 < 3 * E:
                            sp.dma_start(wst[:, k], piece(a["moe"], m + 2)).then_inc(s_wld[k], 16)

                    def body(i, r, q):
                        one, two = (r + 2) % 3, (r + 1) % 3
                        if splits(i, 1):
                            store_weight(i - 1, 1)
                        if valid(i, 1):
                            shift(i - 1, one, 1)
                        if valid(i, -2):
                            load(i + 2, one)
                        if valid(i, 2):
                            if not isinstance(i, int) or i > 2:
                                sp.wait_ge(s_xst, 16 * n(i, 2))
                                apart(sp)
                                if L == 0:
                                    sp.wait_ge(s_xn1, 2 * (i - 2))
                            sp.dma_start(xo, batch_rows(xres, i - 2)).then_inc(s_xo, 16)
                        if valid(i, -1):
                            b = i + 1
                            if L == 1:
                                sp.wait_ge(s_mix, 4 * b + 4)
                                sp.dma_start(batch_rows(x2_d, b), xin[:, two]).then_inc(s_x2, 16)
                            if not isinstance(i, int) or i >= 2:
                                sp.wait_ge(s_t, 16 * (n(b) - 2))
                                apart(sp)
                            if L == 1 and isinstance(i, int) and i < 2:
                                sp.wait_ge(s_t, 16 * B)
                            sp.wait_ge(s_kh, n(b) + 1)
                            apart(sp)
                            sp.wait_ge(s_kl, n(b) + 1)
                            apart(sp)
                            for k, l in ((0, 0), (1, 0), (2, 1)):
                                for ab in range(2):
                                    sp.dma_start(ks[32 * k + 16 * ab:32 * k + 16 * ab + 16, two, ab].rearrange("p a t -> p (a t)"),
                                                 khl[64 * ab:64 * ab + 64, l]).then_inc(s_kst, 16)
                            for ab in range(2):
                                sp.dma_start(ks[KPM:KPM + 1, two, ab], kpm_d[bass.ds(n(b), 1)].unsqueeze(1).broadcast_to([1, PAIRS, S])).then_inc(s_kst, 16)
                            sp.wait_ge(s_qh, n(b) + 1)
                            sp.wait_ge(s_ql, n(b) + 1)
                            for k, l in ((0, 0), (1, 1), (2, 0)):
                                sp.dma_start(qs[32 * k:32 * k + 32, two].rearrange("p a t -> p (a t)"), qhl[:, l]).then_inc(s_qst, 16)
                            if L == 1:
                                sp.wait_ge(s_x2, 16 * b + 16)
                        if splits(i):
                            store_weight(i, 0)
                        if valid(i, 0):
                            shift(i, r, 0)
                        if valid(i, 2):
                            sp.wait_ge(s_x1, n(i, 2) + 1)
                            sp.dma_start(batch_rows(xdst, i - 2), xo).then_inc(s_xst, 16)
                        if L == 0 and isinstance(i, int) and i == 1:
                            for k in range(2):
                                sp.dma_start(wst[:, k], piece(a["moe"], k)).then_inc(s_wld[k], 16)
                    iterations(sp, body)
                    sp.wait_ge(s_xst, 16 * B * (L + 1))
                    if L == 0:
                        for k in range(2):
                            sp.wait_ge(s_wst[k], 16 * 3 * E // 2)
                        sp.wait_ge(s_scat, 64 * B)

                @block.gpsimd
                def _(pool):
                    def reciprocal_deviation(b):
                        pool.wait_ge(s_ln, 4 * n(b) + 4)
                        apart(pool)
                        pool.tensor_scalar(lnrs[:, 0], lnmv[:, :, 1], EPS, None, ALU.add).then_inc(s_var, 1)
                        pool.wait_ge(s_var, n(b) + 1)
                        pool.tensor_tensor(lnrs[:, 1], lnrs[:, 0], mhalf[:], ALU.pow).then_inc(s_rs, 1)

                    def low_weight(i, k):
                        pool.wait_ge(s_wsh, (i - 2) * 4 + 2 * k + 2)
                        pool.tensor_tensor(wsp[:, k, 1], wst[:, k], wsp[:, k, 0], ALU.subtract).then_inc(s_wsl, 1)

                    def body(i, r, q):
                        one, two = (r + 2) % 3, (r + 1) % 3
                        if splits(i, 1):
                            low_weight(i - 1, 1)
                        if L == 1 and valid(i, -2):
                            b = i + 2
                            if not isinstance(i, int) or b > 0:
                                pool.wait_ge(s_mix, 4 * b)
                            pool.tensor_copy(gidx[:].unsqueeze(1), POS[:, bass.ds(b, 1)]).then_inc(s_gi, 1)
                            pool.wait_ge(s_gi, b + 1)
                            apart(pool)
                            for k in range(2):
                                for c in range(C2):
                                    pool.indirect_dma_start(ga[:, k, c], None, y_d[:, :],
                                                            bass.IndirectOffsetOnAxis(ap=gidx[:, 2 * k + c:2 * k + c + 1], axis=0)).then_inc(s_ga, 16)
                        if L == 1 and valid(i, 2):
                            pool.wait_ge(s_xo, 16 * n(i, 2) + 16)
                            apart(pool)
                            pool.tensor_tensor(xo[:], xo[:], bo[:].unsqueeze(1).broadcast_to([P, C2, D]), ALU.add).then_inc(s_bo, 1)
                        if splits(i):
                            low_weight(i, 0)
                        if L == 0 and valid(i, -2):
                            reciprocal_deviation(i + 2)
                        if L == 0 and valid(i, 2):
                            b = i - 2
                            pool.wait_ge(s_l2, 4 * b + 4)
                            apart(pool)
                            pool.tensor_scalar(l2rs[:, 0], l2mv[:, :, 1], EPS, None, ALU.add).then_inc(s_var2, 1)
                            pool.wait_ge(s_var2, b + 1)
                            pool.tensor_tensor(l2rs[:, 1], l2rs[:, 0], mhalf[:], ALU.pow).then_inc(s_rs2, 1)
                        if L == 1 and valid(i, -2):
                            b = i + 2
                            pool.wait_ge(s_x[one], landed(r, q))
                            pool.wait_ge(s_ga, 64 * b + 64)
                            apart(pool)
                            for k in range(2):
                                weight = WAB[:, k, bass.ds(b * 2, C2)].unsqueeze(2).broadcast_to([P, C2, D])
                                pool.tensor_tensor(ga[:, k], ga[:, k], weight, ALU.mult).then_inc(s_mix, 1)
                            for k in range(2):
                                pool.wait_ge(s_mix, 4 * b + 2 + k)
                                apart(pool)
                                pool.tensor_tensor(xin[:, one], xin[:, one], ga[:, k], ALU.add).then_inc(s_mix, 1)
                        if valid(i, -2):
                            pool.wait_ge(s_ch, n(i, -2) + 1)
                            pool.wait_ge(s_c[one], landed(r, q))
                            pool.tensor_tensor(chl[:, 1], cin[:, one], chl[:, 0], ALU.subtract).then_inc(s_cl, 1)
                        if L == 1 and valid(i, -2):
                            reciprocal_deviation(i + 2)
                        if L == 0 and valid(i, 3):
                            b = i - 3
                            pool.wait_ge(s_rt, RT * (b + 1))
                            apart(pool)
                            for k in range(2):
                                for c in range(C2):
                                    pool.indirect_dma_start(routed_d[:, :], bass.IndirectOffsetOnAxis(ap=rowi[:, k, c:c + 1], axis=0),
                                                            xr[:, r, c], None).then_inc(s_scat, 16)
                        if L == 0 and valid(i, 2):
                            b = i - 2
                            pool.wait_ge(s_xrh, b + 1)
                            pool.tensor_tensor(xr[:, two, :, D:2 * D], xn1[:], xr[:, two, :, 0:D], ALU.subtract).then_inc(s_xrl, 1)

                    iterations(pool, body)

                @block.scalar
                def _(act):
                    def body(i, r, q):
                        one, two = (r + 2) % 3, (r + 1) % 3
                        for s in range(16):
                            if s == 1 and valid(i, 2):
                                u_out(i - 2, 1)
                            if valid(i, 1):
                                exp(i - 1, s, head_slot(r, s))
                            if s == 9 and valid(i, 1):
                                u_out(i - 1, 0)
                            if s == at["M1"] and valid(i, 1):
                                maxima(i, i - 1, 1)
                            if s == at["M0"] and valid(i, 0):
                                maxima(i, i, 0)
                            if s == 12 and valid(i, -2):
                                act.wait_ge(s_c[one], landed(r, q))
                                if not isinstance(i, int) or i > -2:
                                    act.wait_ge(s_md, misc.before(i, "V") + 1)
                                act.activation(chl[:, 0], cin[:, one], ACT.Copy).then_inc(s_ch, 1)
                            if s == at["XT"] and valid(i, -1):
                                act.wait_ge(s_md, misc.before(i, "XT") + 1)
                                act.activation(xh, psN.rearrange("p (c n) -> p c n", c=C2), ACT.Copy).then_inc(s_xh, 1)
                            for name, step, dst, done, copied, w in (("Q", at["Q"], qhl, s_qh, s_qst, 48), ("K", at["K"], khl, s_kh, s_kst, 128)):
                                if s == step and valid(i, -1):
                                    act.wait_ge(s_md, misc.before(i, name) + 1)
                                    if not isinstance(i, int) or i >= 0:
                                        act.wait_ge(copied, w * n(i, -1))
                                    if L == 0:
                                        act.activation(dst[:, 0], bank(name), ACT.Copy).then_inc(done, 1)
                                    else:
                                        for g in range(C2):
                                            last = act.activation(dst[:, 0, g * S:(g + 1) * S], bank(name)[:, g * S:(g + 1) * S], ACT.Identity,
                                                                  bias=bqk[:, int(name == "K"), g:g + 1])
                                        last.then_inc(done, 1)
                            if s in SPLIT_STEPS and splits(i):
                                k, stage, half = np.unravel_index(SPLIT_STEPS.index(s), (2, 2, 2))
                                cut = slice(1024 * half, 1024 * half + 1024)
                                if stage == 0:
                                    if half == 0:
                                        act.wait_ge(s_wld[k], 16 * (i - 1))
                                    act.activation(wst[:, k, cut], wst[:, k, cut], ACT.Copy, scale=WSC).then_inc(s_wss, 1)
                                else:
                                    act.wait_ge(s_wss, (i - 2) * 4 + int(2 * k + half + 1))
                                    if half == 0 and (not isinstance(i, int) or i > 2):
                                        act.wait_ge(s_wst[k], 16 * (i - 2))
                                    act.activation(wsp[:, k, 0, cut], wst[:, k, cut], ACT.Copy).then_inc(s_wsh, 1)
                            if s == at["OT"] and valid(i, 2):
                                act.wait_ge(s_md, misc.before(i, "OT") + 1)
                                act.activation(ohl[:, 0], psM[:, :].rearrange("p (c n) -> p c n", c=C2), ACT.Copy).then_inc(s_oh, 1)
                            if L == 0 and s == 15 and valid(i, 2):
                                b = i - 2
                                act.wait_ge(s_xn1, 2 * b + 2)
                                act.activation(xr[:, two, :, 0:D], xn1[:], ACT.Copy).then_inc(s_xrh, 1)
                            if L == 0 and s == at["GT"] and valid(i, 3):
                                act.wait_ge(s_md, misc.before(i, "GT") + 1)
                                act.activation(xg[:].rearrange("p k n -> p (k n)"), psM16, ACT.Copy).then_inc(s_xg, 1)

                    def maxima(i, b, half):
                        act.wait_ge(s_md, misc.before(i, f"M{half}") + 1)
                        if not isinstance(b, int) or n(b) > 0:
                            act.wait_ge(s_sh, 32 * n(b) - 16 + 16 * half)
                        act.activation(mt[:, half], bank(f"M{half}")[0:8, 0:S], ACT.Copy, scale=-1.0 / SHIFT).then_inc(s_mt, 1)

                    def exp(b, s, slot):
                        p = s // 2
                        act.wait_ge(s_t, 16 * n(b) + s + 1)
                        if s % 2 == 0 and (not isinstance(b, int) or 4 * n(b) + p // 2 > 1):
                            act.wait_ge(s_pv, 4 * n(b) + p // 2 - 1)
                        act.activation(pt[:, p % 4, s % 2], psH[:, slot], ACT.Exp, scale=LOGIT).then_inc(s_exp, 1)

                    def u_out(b, half):
                        act.wait_ge(s_pv, 4 * n(b) + 2 * half + 2)
                        if half == 0 and (not isinstance(b, int) or b > 0):
                            act.wait_ge(s_o, 2 * n(b))
                        act.activation(uu[:, half], psU[:, :], ACT.Copy).then_inc(s_u, 1)

                    iterations(act, body)

                @block.vector
                def _(dve):
                    def stats(src, st, mv, done, m):
                        for c in range(C2):
                            dve.bn_stats(st[:, c], src[:, c]).then_inc(done, 1)
                        for c in range(C2):
                            dve.wait_ge(done, 4 * m + c + 1)
                            apart(dve)
                            dve.bn_aggr(mv[:, c], st[:, c]).then_inc(done, 1)

                    def body(i, r, q):
                        one, two = (r + 2) % 3, (r + 1) % 3
                        b = i + 1
                        for s in range(16):
                            if L == 0 and s in (at["RK"] + 1, at["RK"] + 2) and valid(i, 3):
                                rows_of(i, i - 3, 2 * (s - at["RK"] - 1))
                            if valid(i, 0):
                                half, col = s // 8, (s % 2) * 4 + (s % 8) // 2
                                dve.wait_ge(s_s, 16 * n(i) + s + 1)
                                if s % 8 == 0 and (not isinstance(i, int) or i > 0):
                                    dve.wait_ge(s_mt, 2 * n(i) - 1 + half)
                                dve.tensor_reduce(mx[:, half, :, col], psS[:, s % 2].rearrange("p (c n) -> p c n", c=C2), X, ALU.max).then_inc(s_mx, 1)
                            if L == 0 and 4 <= s < 11 and valid(i, 3):
                                choose(i, i - 3, 2 * (s - 4))
                            if L == 0 and 4 <= s < 10 and valid(i, 3):
                                choose(i, i - 3, 2 * (s - 4) + 1)
                            if s == 11 and valid(i, -2):
                                dve.wait_ge(s_x[one], landed(r, q))
                                if L == 1:
                                    dve.wait_ge(s_mix, 4 * i + 12)
                                stats(xin[:, one], lnst, lnmv, s_ln, n(i, -2))
                            if s == 1 and valid(i, -1):
                                dve.wait_ge(s_rs, n(b) + 1)
                                for c in range(C2):
                                    dve.tensor_scalar(xn[:, c], xin[:, two, c], lnmv[:, c, 0:1], lnrs[:, 1, c:c + 1], ALU.subtract, ALU.mult).then_inc(s_xn, 1)
                            if L == 0 and s in (at["RK"] + 1, at["RK"] + 2) and valid(i, 3):
                                rows_of(i, i - 3, 2 * (s - at["RK"] - 1) + 1)
                            if s == at["XT"] + 1 and valid(i, -1):
                                dve.wait_ge(s_xh, n(b) + 1)
                                dve.tensor_tensor(xl, psN.rearrange("p (c n) -> p c n", c=C2), xh, ALU.subtract).then_inc(s_xl, 1)
                            for qc in range(2):
                                if s == at[f"UT{qc}"] + 1 and valid(i, 2):
                                    dve.wait_ge(s_md, misc.before(i, f"UT{qc}") + 1)
                                    heads = psM[:, :].rearrange("p (h k) -> p h k", k=32)
                                    dve.reciprocal(rden[:, qc], heads[:, :, HD]).then_inc(s_rd, 1)
                                    dve.wait_ge(s_rd, 2 * n(i, 2) + qc + 1)
                                    ins = dve.tensor_tensor(oo[:, qc].rearrange("p (h k) -> p h k", k=HD), heads[:, :, 0:HD],
                                                            rden[:, qc].unsqueeze(2).broadcast_to([P, H, HD]), ALU.mult)
                                    ins.then_inc(s_o, 1)
                            for name, step, dst, done, high in (("Q", at["Q"] + 1, qhl, s_ql, s_qh), ("K", at["K"] + 1, khl, s_kl, s_kh)):
                                if s == step and valid(i, -1):
                                    dve.wait_ge(high, n(b) + 1)
                                    if L == 0:
                                        dve.tensor_tensor(dst[:, 1], bank(name), dst[:, 0], ALU.subtract).then_inc(done, 1)
                                    else:
                                        for g in range(C2):
                                            last = dve.scalar_tensor_tensor(out=dst[:, 1, g * S:(g + 1) * S], in0=bank(name)[:, g * S:(g + 1) * S],
                                                                            scalar=bqk[:, int(name == "K"), g:g + 1],
                                                                            in1=dst[:, 0, g * S:(g + 1) * S], op0=ALU.add, op1=ALU.subtract)
                                        last.then_inc(done, 1)
                            if s == at["OT"] + 1 and valid(i, 2):
                                dve.wait_ge(s_oh, n(i, 2) + 1)
                                dve.tensor_tensor(ohl[:, 1], psM[:, :].rearrange("p (c n) -> p c n", c=C2), ohl[:, 0], ALU.subtract).then_inc(s_ol, 1)
                            if s == at["V"] + 1 and valid(i, -1):
                                dve.wait_ge(s_md, misc.before(i, "V") + 1)
                                if not isinstance(i, int) or i >= 2:
                                    dve.wait_ge(s_pv, 4 * (n(b) - 2))
                                for c in range(C2):
                                    last = dve.scalar_tensor_tensor(out=vv[:, two, c, :, 0:HD], in0=psN[:, c * S:(c + 1) * S].rearrange("p (h k) -> p h k", k=HD),
                                                                    scalar=1.0 / WSC, in1=(bv if L else zero)[:].rearrange("p (h k) -> p h k", k=HD),
                                                                    op0=ALU.mult, op1=ALU.add)
                                last.then_inc(s_v, 1)
                            if s == at["WO"] + 1 and valid(i, 2):
                                m = n(i, 2)
                                if L == 0:
                                    dve.wait_ge(s_xo, 16 * m + 16)
                                else:
                                    dve.wait_ge(s_bo, i - 1)
                                dve.wait_ge(s_md, misc.before(i, "WO") + 1)
                                dve.scalar_tensor_tensor(out=xo[:], in0=psM[:, :].rearrange("p (c n) -> p c n", c=C2), scalar=tg64[:, 2 * L:2 * L + 1],
                                                         in1=xo[:], op0=ALU.mult, op1=ALU.add).then_inc(s_x1, 1)
                                if L == 0:
                                    dve.wait_ge(s_x1, m + 1)
                                    stats(xo, l2st, l2mv, s_l2, i - 2)
                            if s == 14 and L == 0 and valid(i, 2):
                                dve.wait_ge(s_rs2, i - 1)
                                if not isinstance(i, int) or i > 2:
                                    dve.wait_ge(s_xrl, i - 2)
                                for c in range(C2):
                                    dve.tensor_scalar(xn1[:, c], xo[:, c], l2mv[:, c, 0:1], l2rs[:, 1, c:c + 1], ALU.subtract, ALU.mult).then_inc(s_xn1, 1)

                    def choose(i, b, k):
                        wide = [P, C2, E]
                        w8b = w8[:].unsqueeze(1).broadcast_to(wide)
                        if k == 0:
                            dve.wait_ge(s_md, misc.before(i, "GS") + 1)
                            ins = dve.tensor_scalar(sc[:, 0], psM[:, 0:C2 * E].rearrange("p (c e) -> p c e", c=C2), 1.0 / WSC, None, ALU.mult)
                        else:
                            dve.wait_ge(s_rt, RT * b + k)
                            again, stage = (k - 1) // 6, (k - 1) % 6
                            if k == 12:
                                dve.tensor_copy(OH[:, bass.ds(b, 1)], oh[:].rearrange("p k c e -> p (k c e)").unsqueeze(1))
                                dve.tensor_copy(TOP[:, bass.ds(b, 1)], top[:].rearrange("p k c -> p (k c)").unsqueeze(1))
                                ins = dve.tensor_tensor(chosen[:], oh[:, 0], oh[:, 1], ALU.add)
                            elif stage == 0:
                                ins = dve.tensor_reduce(top[:, again], sc[:, again], X, ALU.max)
                            elif stage == 1:
                                ins = dve.tensor_tensor(eqm[:], sc[:, again], top[:, again].unsqueeze(2).broadcast_to(wide), ALU.is_equal)
                            elif stage == 2:
                                ins = dve.tensor_tensor(eqm[:], eqm[:], w8b, ALU.mult)
                            elif stage == 3:
                                ins = dve.tensor_reduce(wmax[:], eqm[:], X, ALU.max)
                            elif stage == 4:
                                ins = dve.tensor_tensor(oh[:, again], w8b, wmax[:].unsqueeze(2).broadcast_to(wide), ALU.is_equal)
                            else:
                                ins = dve.scalar_tensor_tensor(out=sc[:, 1], in0=oh[:, 0], scalar=-1e30, in1=sc[:, 0], op0=ALU.mult, op1=ALU.add)
                        ins.then_inc(s_rt, 1)

                    def rows_of(i, b, k):
                        base = RT * b + 13
                        if k == 0:
                            dve.wait_ge(s_md, misc.before(i, "RK") + 1)
                            dve.tensor_tensor(rank[:], psN[:, 0:C2 * E].rearrange("p (c e) -> p c e", c=C2), runb[:].unsqueeze(1).broadcast_to([P, C2, E]), ALU.add).then_inc(s_rt, 1)
                        if k == 1:
                            dve.wait_ge(s_rt, base + 1)
                            for choice in range(2):
                                last = dve.tensor_tensor(prod[:, choice], oh[:, choice], rank[:], ALU.mult)
                            last.then_inc(s_rt, 1)
                            dve.tensor_tensor(runb[:], psN[:, C2 * E:C2 * E + E], runb[:], ALU.add).then_inc(s_rt, 1)
                        if k == 2:
                            dve.wait_ge(s_rt, base + 3)
                            dve.tensor_reduce(row[:], prod[:], X, ALU.add).then_inc(s_rt, 1)
                        if k == 3:
                            dve.wait_ge(s_rt, base + 4)
                            if not isinstance(i, int) or b > 0:
                                dve.wait_ge(s_scat, 64 * b)
                            dve.tensor_copy(ROW[:, bass.ds(b, 1)], row[:].rearrange("p k c -> p (k c)").unsqueeze(1))
                            dve.tensor_copy(rowi[:], row[:]).then_inc(s_rt, 1)

                    iterations(dve, body)

                @block.tensor
                def _(pe):
                    def proj(dst, stat, mov):
                        for c in range(C2):
                            for ls, lm in ((0, 0), (0, 1), (1, 0)):
                                last = pe.matmul(dst, stat(ls, c), mov(lm, c), start=(c == 0 and (ls, lm) == (0, 0)), stop=(c == C2 - 1 and ls == 1))
                        return last

                    def free(i, name):
                        front = misc.previous(i, name)
                        if front is None:
                            return
                        k, name = front
                        m = k - misc.lag[name]
                        done, value = {
                            "M0": (s_mt, 2 * n(m) + 1), "M1": (s_mt, 2 * n(m) + 2), "XT": (s_xl, n(m) + 1),
                            "UT0": (s_o, 2 * n(m) + 1), "UT1": (s_o, 2 * n(m) + 2), "Q": (s_ql, n(m) + 1), "K": (s_kl, n(m) + 1),
                            "V": (s_v, n(m) + 1), "OT": (s_ol, n(m) + 1), "WO": (s_x1, n(m) + 1), "GT": (s_xg, n(m) + 1),
                            "GS": (s_rt, RT * m + 1), "RK": (s_rt, RT * m + 16),
                        }[name]
                        pe.wait_ge(done, value)

                    def pv(b, g, slot):
                        pe.wait_ge(s_exp, 16 * n(b) + 4 * g + 4)
                        pe.wait_ge(s_v, n(b) + 1)
                        if g % 2 == 0 and (not isinstance(b, int) or n(b) > 0 or g > 0):
                            pe.wait_ge(s_u, 2 * n(b) + g // 2)
                        for kc in range(C2):
                            for j in range(4):
                                h = 4 * g + j
                                last = pe.matmul(psU[32 * j:32 * j + 32, (g % 2) * S:(g % 2 + 1) * S], vv[:, slot, kc, h],
                                                 pt[:, (h // 2) % 4, h % 2, kc * S:(kc + 1) * S], start=(kc == 0), stop=(kc == C2 - 1))
                        last.then_inc(s_pv, 1)

                    def body(i, r, q):
                        one, two = (r + 2) % 3, (r + 1) % 3
                        b = i + 1
                        for s in range(16):
                            h, p = s, s // 2
                            if valid(i, 0):
                                if s == 0:
                                    pe.wait_ge(s_qst, 48 * n(i) + 48)
                                    pe.wait_ge(s_kst, 128 * n(i) + 128)
                                if not isinstance(i, int) or 16 * n(i) + s > 1:
                                    pe.wait_ge(s_mx, 16 * n(i) + s - 1)
                                if L == 0:
                                    pe.matmul(psS[:, s % 2], idmask[:], maskh[:].rearrange("p c n -> p (c n)"), start=True, stop=False, skip_group_check=True)
                                for qc in range(C2):
                                    last = pe.matmul(psS[:, s % 2, qc * S:(qc + 1) * S], qs[0:SHA, r, p, qc * P:(qc + 1) * P], ks[0:SHA, r, s % 2, p],
                                                     start=(L == 1), stop=True, skip_group_check=True)
                                last.then_inc(s_s, 1)
                            if valid(i, 1):
                                if s % 8 == 0:
                                    pe.wait_ge(s_sh, 32 * n(i, 1) + 16 + 16 * (s // 8))
                                if not isinstance(i, int) or 16 * (i - 1) + s > 2:
                                    pe.wait_ge(s_exp, 16 * n(i, 1) + s - 2)
                                if L == 0:
                                    for l in range(2):
                                        pe.matmul(psH[:, head_slot(r, s)], idmask[:], maskThl[:, l].rearrange("p c n -> p (c n)"), start=(l == 0), stop=False,
                                                  skip_group_check=True)
                                for kc in range(C2):
                                    last = pe.matmul(psH[:, head_slot(r, s), kc * S:(kc + 1) * S], ks[0:STACK, one, s % 2, p, kc * P:(kc + 1) * P],
                                                     qs[0:STACK, one, p], start=(L == 1), stop=True, skip_group_check=True)
                                last.then_inc(s_t, 1)
                            if s == 1 and valid(i, 2):
                                pv(i - 2, 3, two)
                            if s in (5, 9, 13) and valid(i, 1):
                                pv(i - 1, s // 4 - 1, one)
                            name = misc.steps.get(s)
                            if name is None or not valid(i, misc.lag[name]):
                                continue
                            free(i, name)
                            if name in ("M0", "M1"):
                                half, m = int(name[1]), i - misc.lag[name]
                                pe.wait_ge(s_mx, 16 * n(m) + 8 * half + 8)
                                for qc in range(C2):
                                    last = pe.transpose(bank(name)[0:8, qc * P:(qc + 1) * P], mx[:, half, qc], id32[:])
                            elif name == "XT":
                                pe.wait_ge(s_xn, 2 * n(b) + 2)
                                for c in range(C2):
                                    for t in range(C2):
                                        last = pe.transpose(psN[:, c * S + t * P:c * S + (t + 1) * P], xn[:, t, c * P:(c + 1) * P], id32[:])
                            elif name == "Q":
                                pe.wait_ge(s_xl, n(b) + 1)
                                for g in range(C2):
                                    last = proj(psN[:, g * S:(g + 1) * S], lambda l, c: aw[:, L, l, 0, c, g * P:(g + 1) * P], lambda l, c: xhl[:, l, c])
                            elif name == "K":
                                pe.wait_ge(s_cl, n(b) + 1)
                                for g in range(C2):
                                    last = proj(psN[:, g * S:(g + 1) * S], lambda l, c: aw[:, L, l, 1, c, g * P:(g + 1) * P], lambda l, c: chl[:, l, c])
                            elif name == "V":
                                for t in range(C2):
                                    last = proj(psN[:, t * S:(t + 1) * S], lambda l, c: chl[:, l, c, t * P:(t + 1) * P], lambda l, c: aw[:, L, l, 2, c])
                            elif name in ("UT0", "UT1"):
                                qc = int(name[2])
                                pe.wait_ge(s_u, 2 * n(i, 2) + 2)
                                for g in range(4):
                                    last = pe.transpose(psM[:, g * P:(g + 1) * P], uu[:, g // 2, (g % 2) * S + qc * P:(g % 2) * S + (qc + 1) * P], id32[:])
                            elif name == "OT":
                                pe.wait_ge(s_o, 2 * n(i, 2) + 2)
                                for c in range(C2):
                                    for t in range(C2):
                                        last = pe.transpose(psM[:, c * S + t * P:c * S + (t + 1) * P], oo[:, t, c * P:(c + 1) * P], id32[:])
                            elif name == "WO":
                                pe.wait_ge(s_ol, n(i, 2) + 1)
                                for t in range(C2):
                                    last = proj(psM[:, t * S:(t + 1) * S], lambda l, c: ohl[:, l, c, t * P:(t + 1) * P], lambda l, c: aw[:, L, l, 3, c])
                            elif name == "GT":
                                pe.wait_ge(s_xrl, i - 2)
                                for l in range(2):
                                    for c in range(C2):
                                        for t in range(C2):
                                            at_ = (2 * l + c) * S + t * P
                                            last = pe.transpose(psM16[:, at_:at_ + P], xr[:, r, t, l * D + c * P:l * D + (c + 1) * P], id16[:])
                            elif name == "GS":
                                pe.wait_ge(s_xg, i - 2)
                                for t in range(C2):
                                    last = proj(psM[:, t * E:(t + 1) * E], lambda l, c: xg[:, 2 * l + c, t * P:(t + 1) * P], lambda l, c: gatehl[:, l, c])
                            elif name == "RK":
                                pe.wait_ge(s_rt, RT * (i - 3) + 13)
                                pe.matmul(psN[:, 0:E], lower[:], chosen[:, 0], start=True, stop=True)
                                pe.matmul(psN[:, E:2 * E], lower[:], chosen[:, 1], start=True, stop=False)
                                pe.matmul(psN[:, E:2 * E], ones16[:], chosen[:, 0], start=False, stop=True)
                                pe.matmul(psN[:, 2 * E:3 * E], ones16[:], chosen[:, 0], start=True, stop=False)
                                last = pe.matmul(psN[:, 2 * E:3 * E], ones16[:], chosen[:, 1], start=False, stop=True)
                            last.then_inc(s_md, 1)

                    iterations(pe, body)

        attention(0)

        with nc.Block() as block:
            w13 = big[:, :, 0:2].rearrange("p s w l (c n) -> p s w l c n", c=C2)
            w2 = big[:, :, 2].rearrange("p s l (c n) -> p s l c n", c=NI)

            @block.sync
            def _(sp):
                sp.wait_ge(s_end, 1)
                for e in range(E):
                    first = sp.value_load(endi[0:1, e:e + 1], min_val=0, max_val=E * REGION - TILE)
                    sp.dma_start(routed_d[bass.ds(first, TILE)].rearrange("(c p) n -> p c n", p=P), zero16[:]).then_inc(s_zf, 16)

                def rows(t, slot):
                    first = sp.value_load(rowt[0:1, bass.ds(t, 1)], min_val=0, max_val=E * REGION - TILE)
                    sp.dma_start(mxr[:, slot], routed_d[bass.ds(first, TILE)].rearrange("(c p) n -> p c n", p=P)).then_inc(s_mr[slot], 16)

                def weights(t, slot, js):
                    e3 = sp.value_load(eidt[0:1, bass.ds(t, 1)], min_val=0, max_val=3 * E - 3)
                    for j in js:
                        sp.dma_start(big[:, slot, j].rearrange("p l n -> p (l n)"), ws_d[bass.ds(e3 + j, 1)].rearrange("o p n -> (o p) n")).then_inc((s_w2 if j == 2 else s_w13)[slot], 16)

                def tile(t, slot, more=True):
                    if more:
                        sp.wait_ge(s_xtp, t + 1)
                        rows(t + 2, slot)
                        sp.wait_ge(s_h, 4 * t + 4)
                        apart(sp)
                        weights(t + 2, slot, (0, 1))
                    sp.wait_ge(s_ye, t + 1)
                    sp.dma_start(y_d[bass.ds(t * TILE, TILE)].rearrange("(c p) d -> p c d", p=P), ye[:, slot].rearrange("p (c d) -> p c d", c=C2)).then_inc(s_yst[slot], 16)
                    if more:
                        weights(t + 2, slot, (2,))

                sp.wait_ge(s_tab, 1)
                for t in range(2):
                    weights(t, t, (0, 1))
                    if t == 0:
                        sp.wait_ge(s_zf, 16 * E)
                    rows(t, t)
                    weights(t, t, (2,))
                for t in range(3):
                    tile(t, t % 2)
                with sp.Fori(0, (NT - 5) // 2) as j:
                    for r in range(2):
                        tile(j * 2 + (3 + r), (3 + r) % 2)
                for t in range(NT - 2, NT):
                    tile(t, t % 2, more=False)
                for slot in range(2):
                    sp.wait_ge(s_yst[slot], 16 * len(range(slot, NT, 2)))

            @block.gpsimd
            def _(pool):
                pool.iota(tt[:], [[1, NT]], base=0, channel_multiplier=0, allow_small_or_imprecise_dtypes=True).then_inc(s_tt, 1)
                for k in range(3):
                    if k:
                        pool.wait_ge(s_fq, k)
                    pool.dma_start(fst[:], a["fw"][k]).then_inc(s_fw, 16)

            @block.vector
            def _(dve):
                k = [0]

                def step(ins):
                    k[0] += 1
                    ins.then_inc(s_rf, 1)
                    dve.wait_ge(s_rf, k[0])

                dve.tensor_copy(endi[:], runb[:]).then_inc(s_end, 1)
                for e in range(E):
                    last = dve.tensor_scalar(cnt[:, e:e + 1], runb[:, e:e + 1], -float(e * REGION), None, ALU.add)
                step(last)
                step(dve.tensor_scalar(ntile[:], cnt[:], 1.0 / TILE, 0.5 - 0.5 / TILE, ALU.mult, ALU.add))
                step(dve.tensor_scalar(ntile[:], ntile[:], RND, None, ALU.add))
                step(dve.tensor_scalar(ntile[:], ntile[:], RND, None, ALU.subtract))
                step(dve.memset(cum[:], 0.0))
                src = ntile[:]
                for shift_, dst in ((1, scan[:, 0]), (2, scan[:, 1]), (4, cum[:, 1:E + 1])):
                    dve.tensor_copy(dst[:, 0:shift_], src[:, 0:shift_])
                    step(dve.tensor_tensor(dst[:, shift_:E], src[:, shift_:E], src[:, 0:E - shift_], ALU.add))
                    src = dst
                step(dve.tensor_scalar(base[:], cum[:, 0:E], -float(TILE), None, ALU.mult))
                for e in range(1, E):
                    last = dve.tensor_scalar(base[:, e:e + 1], base[:, e:e + 1], float(e * REGION), None, ALU.add)
                step(last)
                step(dve.tensor_scalar(delta[:], base[:], -1.0, None, ALU.mult))
                step(dve.tensor_tensor(dbase[:], base[:, 1:E], base[:, 0:E - 1], ALU.subtract))
                step(dve.tensor_scalar(lim[:], ntile[:, E - 1:E], -1.0, 0.0, ALU.add, ALU.max))
                step(dve.tensor_scalar(lim[:], lim[:], float(TILE), float((E - 1) * REGION), ALU.mult, ALU.add))
                dve.wait_ge(s_tt, 1)
                step(dve.tensor_scalar(rowf[:], tt[:], float(TILE), None, ALU.mult))
                table = [P, NT, E - 1]
                step(dve.tensor_tensor(ge[:], tt[:].unsqueeze(2).broadcast_to(table), cum[:, 1:E].unsqueeze(1).broadcast_to(table), ALU.is_ge))
                dve.tensor_reduce(eid[:], ge[:], X, ALU.add)
                step(dve.tensor_tensor(gd[:], ge[:], dbase[:].unsqueeze(1).broadcast_to(table), ALU.mult))
                step(dve.tensor_reduce(gs[:], gd[:], X, ALU.add))
                step(dve.tensor_tensor(rowf[:], rowf[:], gs[:], ALU.add))
                step(dve.tensor_scalar(rowf[:], rowf[:], lim[:, 0:1], None, ALU.min))
                dve.tensor_copy(rowt[:], rowf[:])
                dve.tensor_scalar(eidt[:], eid[:], 3.0, None, ALU.mult).then_inc(s_tab, 1)
                wide = OH[:, :, :].rearrange("p b k -> p (b k)").rearrange("p (n e) -> p n e", e=E)
                step(dve.tensor_tensor(wide, wide, delta[:].unsqueeze(1).broadcast_to([P, 4 * B, E]), ALU.mult))
                step(dve.tensor_reduce(posf[:], wide, X, ALU.add))
                rows_ = ROW[:, :, :].rearrange("p b k -> p (b k)")
                dve.tensor_tensor(POS[:, :, :].rearrange("p b k -> p (b k)"), posf[:], rows_, ALU.add)
                tops = TOP[:, :, :].rearrange("p b (k c) -> p k b c", k=2)
                step(dve.tensor_tensor(tdif[:].rearrange("p (b c) -> p b c", c=C2), tops[:, 1], tops[:, 0], ALU.subtract))
                dve.wait_ge(s_te, 1)
                step(dve.tensor_scalar(tsum[:], tdif[:], 1.0, None, ALU.add))
                step(dve.reciprocal(tsum[:], tsum[:]))
                step(dve.tensor_scalar(WAB[:, 0], tsum[:], tg[:, 1:2], None, ALU.mult))
                dve.tensor_tensor(WAB[:, 1], WAB[:, 0], tdif[:], ALU.mult)

                def turned(t, slot):
                    dve.wait_ge(s_xtp, t + 1)
                    dve.tensor_copy(mxt[:, slot].rearrange("p k n -> p (k n)"), psM16).then_inc(s_xt, 1)

                def tile(t, slot, weight=False, last=False):
                    for p in range(4):
                        if weight and p == 1:
                            magnitudes(t)
                        if p == 2 and not last:
                            turned(t + 1, 1 - slot)
                        dve.wait_ge(s_sg, 4 * t + p + 1)
                        dve.scalar_tensor_tensor(out=hb[:, p % 2], in0=psT[:, p % 2, 1], scalar=1.0 / WSC, in1=sg[:, p % 2], op0=ALU.mult, op1=ALU.mult).then_inc(s_hb, 1)
                        dve.wait_ge(s_hh, 4 * t + p + 1)
                        dve.tensor_tensor(hhl[:, slot, 1, 2 * p:2 * p + 2].rearrange("p c n -> p (c n)"), hb[:, p % 2],
                                          hhl[:, slot, 0, 2 * p:2 * p + 2].rearrange("p c n -> p (c n)"), ALU.subtract).then_inc(s_hl, 1)
                        if weight and p > 1:
                            ternary(t, p - 2)

                def magnitudes(k):
                    dve.wait_ge(s_fw, 16 * k + 16)
                    dve.tensor_reduce(fabs[:, k:k + 1], fst[:], X, ALU.add, apply_absolute_value=True).then_inc(s_fa, 1)

                def ternary(k, half):
                    f = [3 * half]

                    def step(ins):
                        f[0] += 1
                        ins.then_inc(s_ft, 1)
                        dve.wait_ge(s_ft, 5 * k + f[0])
                    if half == 0:
                        dve.wait_ge(s_fr, k + 1)
                        step(dve.tensor_scalar(fmean[:, k:k + 1], psU[:, k:k + 1], 1.0 / (P * 2048), EPS, ALU.mult, ALU.max))
                        step(dve.reciprocal(fscale[:, k:k + 1], fmean[:, k:k + 1]))
                        step(dve.tensor_scalar(fst[:], fst[:], fscale[:, k:k + 1], RND, ALU.mult, ALU.add))
                        return
                    step(dve.tensor_scalar(fst[:], fst[:], RND, 1.0, ALU.subtract, ALU.min))
                    step(dve.tensor_scalar(fwt[:, k], fst[:], -1.0, None, ALU.max))
                    dve.sem_inc(s_fq, 1)

                turned(0, 0)
                for t in range(3):
                    tile(t, t % 2, weight=True)
                with dve.Fori(0, (NT - 5) // 2) as j:
                    for r in range(2):
                        tile(j * 2 + (3 + r), (3 + r) % 2)
                for t in range(NT - 2, NT):
                    tile(t, t % 2, last=t == NT - 1)

            @block.scalar
            def _(act):
                act.wait_ge(s_rf, RF_TDIF)
                act.activation(tdif[:], tdif[:], ACT.Exp).then_inc(s_te, 1)

                def tile(t, slot, first=False):
                    for p in range(4):
                        act.wait_ge(s_h, 4 * t + p + 1)
                        if not (first and p < 2):
                            act.wait_ge(s_hb, 4 * t + p - 1)
                        act.activation(sg[:, p % 2], psT[:, p % 2, 0], ACT.Silu, scale=1.0 / WSC).then_inc(s_sg, 1)
                        act.wait_ge(s_hb, 4 * t + p + 1)
                        if p == 0 and (not isinstance(t, int) or t > 1):
                            act.wait_ge(s_y, t - 1)
                        act.activation(hhl[:, slot, 0, 2 * p:2 * p + 2].rearrange("p c n -> p (c n)"), hb[:, p % 2], ACT.Copy).then_inc(s_hh, 1)
                        if p == 1 and (not isinstance(t, int) or t > 0):
                            out_tile(t - 1, 1 - slot)

                def out_tile(t, slot):
                    act.wait_ge(s_y, t + 1)
                    if not isinstance(t, int) or t > 1:
                        act.wait_ge(s_yst[slot], yturn(t, slot))
                    act.activation(ye[:, slot], psS[:, slot], ACT.Copy, scale=1.0 / WSC).then_inc(s_ye, 1)

                turn = [0]

                def yturn(t, slot):
                    if isinstance(t, int):
                        return 16 * (t // 2)
                    return turn[0]

                for t in range(3):
                    tile(t, t % 2, first=t == 0)
                with act.Fori(0, (NT - 3) // 2) as j:
                    for r in range(2):
                        turn[0] = (j + 1) * 16
                        tile(j * 2 + (3 + r), (3 + r) % 2)
                out_tile(NT - 1, (NT - 1) % 2)

            @block.tensor
            def _(pe):
                def turned(t, slot):
                    pe.wait_ge(s_mr[slot], mturn(t))
                    if not isinstance(t, int) or t > 0:
                        pe.wait_ge(s_xt, t)
                    for l in range(2):
                        for c in range(C2):
                            for h in range(C2):
                                at_ = (2 * l + c) * TILE + h * P
                                last = pe.transpose(psM16[:, at_:at_ + P], mxr[:, slot, h, l * D + c * P:l * D + (c + 1) * P], id16[:])
                    last.then_inc(s_xtp, 1)

                jv = [None]

                def mturn(t):
                    if isinstance(t, int):
                        return 16 * (t // 2 + 1)
                    return jv[0]

                def first_products(t, slot, p):
                    if p == 0:
                        pe.wait_ge(s_xt, t + 1)
                        pe.wait_ge(s_w13[slot], wturn(t) * 2)
                    if not isinstance(t, int) or 4 * t + p > 1:
                        pe.wait_ge(s_hb, 4 * t + p - 1)
                    for cc in range(2):
                        inner = (2 * p + cc) * P
                        for w in range(2):
                            for c in range(C2):
                                for lw, lx in ((0, 0), (0, 1), (1, 0)):
                                    last = pe.matmul(psT[:, p % 2, w, cc * TILE:(cc + 1) * TILE], w13[:, slot, w, lw, c, inner:inner + P],
                                                     mxt[:, slot, 2 * lx + c], start=(c == 0 and lw + lx == 0), stop=(c == 1 and lw == 1))
                    last.then_inc(s_h, 1)

                def second_products(t, slot):
                    pe.wait_ge(s_hl, 4 * t + 4)
                    pe.wait_ge(s_w2[slot], w2turn(t))
                    if not isinstance(t, int) or t > 1:
                        pe.wait_ge(s_ye, t - 1)
                    for h in range(C2):
                        for c in range(NI):
                            for lh, lw in ((0, 0), (0, 1), (1, 0)):
                                last = pe.matmul(psS[:, slot, h * D:(h + 1) * D], hhl[:, slot, lh, c, h * P:(h + 1) * P], w2[:, slot, lw, c],
                                                 start=(c == 0 and lh + lw == 0), stop=(c == NI - 1 and lh == 1))
                    last.then_inc(s_y, 1)

                wv, w2v = [None], [None]

                def wturn(t):
                    return 16 * (t // 2 + 1) if isinstance(t, int) else wv[0]

                def w2turn(t):
                    return 16 * (t // 2 + 1) if isinstance(t, int) else w2v[0]

                def tile(t, slot, weight=False, last=False):
                    first_products(t, slot, 0)
                    if not isinstance(t, int) or t > 0:
                        second_products(t - 1, 1 - slot)
                    first_products(t, slot, 1)
                    first_products(t, slot, 2)
                    if weight:
                        pe.wait_ge(s_fa, t + 1)
                        pe.matmul(psU[:, t:t + 1], ones32[:], fabs[:, t:t + 1], start=True, stop=True).then_inc(s_fr, 1)
                    if not last:
                        turned(t + 1, 1 - slot)
                    first_products(t, slot, 3)

                turned(0, 0)
                for t in range(3):
                    tile(t, t % 2, weight=True)
                with pe.Fori(0, (NT - 5) // 2) as j:
                    for r in range(2):
                        wv[0] = (j + (3 + r) // 2 + 1) * 16
                        w2v[0] = (j + 2) * 16
                        jv[0] = (j + 3) * 16
                        tile(j * 2 + (3 + r), (3 + r) % 2)
                tile(NT - 2, (NT - 2) % 2)
                tile(NT - 1, (NT - 1) % 2, last=True)
                second_products(NT - 1, (NT - 1) % 2)

        attention(1)

        with nc.Block() as block:
            at[0] = 0
            xf = part(4 * D).rearrange("p (s n) -> p s n", s=4)
            xs = part(2 * D).rearrange("p (s n) -> p s n", s=2)
            xnf = part(D)
            q1f = part(D)
            q1 = part(D // 2).bitcast(BF16)
            q1t = part(D).bitcast(BF16).rearrange("p (s n) -> p s n", s=2)
            sgf = part(1024).rearrange("p (s n) -> p s n", s=2)
            hbf = part(INNER)
            q2 = part(INNER).bitcast(BF16).rearrange("p (s n) -> p s n", s=2)
            q2t = part(INNER // 2).bitcast(BF16)
            of = part(2 * D).rearrange("p (s n) -> p s n", s=2)
            psM_b, psU_b = psM[:, :].bitcast(BF16), psU[:, :].bitcast(BF16)
            NU = TOK // P
            F1, F2 = 4, 3

            def tiles(body):
                def run(eng):
                    for u in range(2):
                        body(u, 0)
                    with eng.Fori(0, NU // 4 - 2) as j:
                        for r in range(4):
                            body(2 + r, j)
                    for u in range(NU - 6, NU):
                        body(u, 0)
                return run

            def static(j):
                return isinstance(j, int)

            def num(s, j, off=0):
                return s + off if static(j) else j * 4 + (s + off)

            def some(s, j, off):
                return not static(j) or 0 <= s + off < NU

            def part_of(s, j, off, k):
                return (s + off) // k if static(j) else j * (4 // k) + (s + off) // k

            @block.sync
            def _(sp):
                def load(s, j, off):
                    sp.dma_start(xf[:, (s + off) % 4], x3_d[bass.ds(num(s, j, off) * P, P)]).then_inc(s_xf[(s + off) % 4], 16)

                def body(s, j):
                    if some(s, j, 4):
                        sp.wait_ge(s_xnf, num(s, j, 1))
                        apart(sp)
                        load(s, j, 4)
                    if not static(j) or s > 1:
                        sp.wait_ge(s_res, num(s, j, -1))
                        apart(sp)
                    sp.dma_start(xs[:, s % 2], x3_d[bass.ds(num(s, j) * P, P)]).then_inc(s_xs[s % 2], 16)
                    if some(s, j, -1):
                        store(s, j, -1)

                def store(s, j, off):
                    sp.wait_ge(s_res, num(s, j, off) + 1)
                    apart(sp)
                    sp.dma_start(out[bass.ds(num(s, j, off) * P, P)], of[:, (s + off) % 2]).then_inc(s_ost[(s + off) % 2], 16)

                for u in range(4):
                    load(u, 0, 0)
                tiles(body)(sp)
                store(NU - 1, 0, 0)
                for k in range(2):
                    sp.wait_ge(s_ost[k], 16 * (NU // 2))

            @block.gpsimd
            def _(pool):
                def front(s, j, off):
                    v = num(s, j, off)
                    pool.wait_ge(s_st, 2 * v + 2)
                    apart(pool)
                    pool.tensor_scalar(frs[:, 0:1], fmv[:, 1:2], EPS, None, ALU.add).then_inc(s_fv, 1)
                    pool.wait_ge(s_fv, v + 1)
                    pool.tensor_tensor(frs[:, 1:2], frs[:, 0:1], mhalf[:, 0:1], ALU.pow).then_inc(s_frs, 1)
                    pool.wait_ge(s_frs, v + 1)
                    apart(pool)
                    pool.tensor_scalar(xnf[:], xf[:, (s + off) % 4], fmv[:, 0:1], frs[:, 1:2], ALU.subtract, ALU.mult).then_inc(s_xnf, 1)
                    pool.wait_ge(s_f1, F1 * v + 4)
                    if not static(j) or s + off > 0:
                        pool.wait_ge(s_q1t, v)
                    apart(pool)
                    pool.tensor_scalar(q1[:], q1f[:], RND, None, ALU.subtract).then_inc(s_q1, 1)

                front(0, 0, 0)
                front(1, 0, 0)

                def body(s, j):
                    if some(s, j, 2):
                        front(s, j, 2)

                tiles(body)(pool)

            @block.scalar
            def _(act):
                def silu(s, j, off):
                    v = num(s, j, off)
                    for hf in range(2):
                        act.wait_ge(s_gu, 2 * v + hf + 1)
                        act.activation(sgf[:, hf], psT[:, hf, 0], ACT.Silu, scale=fsc[:, (s + off) % 2, 0:1]).then_inc(s_sil, 1)

                def turned(v):
                    act.wait_ge(s_q2p, v + 1)
                    act.activation(q2t[:], psU_b, ACT.Copy).then_inc(s_q2t, 1)

                def body(s, j):
                    if some(s, j, -1):
                        turned(num(s, j, -1))
                    act.wait_ge(s_f2, F2 * num(s, j) + 3)
                    act.activation(hbf[:], hbf[:], ACT.Identity, bias=rnd[:, 0:1], scale=am[:, 3:4]).then_inc(s_q2a, 1)
                    if some(s, j, 1):
                        silu(s, j, 1)

                silu(0, 0, 0)
                tiles(body)(act)
                turned(NU - 1)

            @block.vector
            def _(dve):
                def stats(s, j, off):
                    dve.wait_ge(s_xf[(s + off) % 4], 16 * part_of(s, j, off, 4) + 16)
                    dve.bn_stats(fst6[:], xf[:, (s + off) % 4]).then_inc(s_st, 1)

                def moments(s, j, off):
                    dve.wait_ge(s_st, 2 * num(s, j, off) + 1)
                    apart(dve)
                    dve.bn_aggr(fmv[:], fst6[:]).then_inc(s_st, 1)

                def first(s, j, off, k):
                    v = num(s, j, off)
                    if k == 0:
                        dve.wait_ge(s_xnf, v + 1)
                        ins = dve.tensor_reduce(am[:, 0:1], xnf[:], X, ALU.max, apply_absolute_value=True)
                    else:
                        dve.wait_ge(s_f1, F1 * v + k)
                    if k == 1:
                        ins = dve.tensor_scalar(am[:, 0:1], am[:, 0:1], 1.0 / 127.0, EPS / 127.0, ALU.mult, ALU.max)
                    if k == 2:
                        dve.tensor_scalar(fsc[:, (s + off) % 2], fmean[:, 0:2], am[:, 0:1], None, ALU.mult)
                        ins = dve.reciprocal(am[:, 1:2], am[:, 0:1])
                    if k == 3:
                        ins = dve.tensor_scalar(q1f[:], xnf[:], am[:, 1:2], RND, ALU.mult, ALU.add)
                    ins.then_inc(s_f1, 1)

                def second(s, j, k):
                    u = num(s, j)
                    if k == 0:
                        dve.wait_ge(s_hm, 2 * u + 2)
                        ins = dve.tensor_reduce(am[:, 2:3], hbf[:], X, ALU.max, apply_absolute_value=True)
                    else:
                        dve.wait_ge(s_f2, F2 * u + k)
                    if k == 1:
                        ins = dve.tensor_scalar(am[:, 2:3], am[:, 2:3], 1.0 / 127.0, EPS / 127.0, ALU.mult, ALU.max)
                    if k == 2:
                        dve.tensor_scalar(fd[:, s % 2:s % 2 + 1], am[:, 2:3], fmean[:, 2:3], tg[:, 3:4], ALU.mult, ALU.mult)
                        ins = dve.reciprocal(am[:, 3:4], am[:, 2:3])
                    ins.then_inc(s_f2, 1)

                def q1_turned(s, j, off):
                    dve.wait_ge(s_q1p, num(s, j, off) + 1)
                    dve.tensor_copy(q1t[:, (s + off) % 2], psM_b[:, 0:D]).then_inc(s_q1t, 1)

                def residual(s, j, off):
                    slot = (s + off) % 2
                    dve.wait_ge(s_dn, num(s, j, off) + 1)
                    dve.wait_ge(s_xs[slot], 16 * part_of(s, j, off, 2) + 16)
                    if not static(j) or s + off > 1:
                        dve.wait_ge(s_ost[slot], 16 * part_of(s, j, off, 2))
                    dve.scalar_tensor_tensor(out=of[:, slot], in0=psS[:, slot, 0:D], scalar=fd[:, slot:slot + 1],
                                             in1=xs[:, slot], op0=ALU.mult, op1=ALU.add).then_inc(s_res, 1)

                def body(s, j):
                    u = num(s, j)
                    if some(s, j, -1):
                        dve.wait_ge(s_q2, u)
                    for hf in range(2):
                        dve.wait_ge(s_sil, 2 * u + hf + 1)
                        dve.scalar_tensor_tensor(out=hbf[:, hf * 512:(hf + 1) * 512], in0=psT[:, hf, 1], scalar=fsc[:, s % 2, 1:2], in1=sgf[:, hf],
                                                 op0=ALU.mult, op1=ALU.mult).then_inc(s_hm, 1)
                    for k in range(3):
                        second(s, j, k)
                        if some(s, j, 2):
                            first(s, j, 2, k)
                    if some(s, j, 3):
                        stats(s, j, 3)
                    if some(s, j, 2):
                        first(s, j, 2, 3)
                    dve.wait_ge(s_q2a, u + 1)
                    dve.tensor_scalar(q2[:, s % 2], hbf[:], RND, None, ALU.subtract).then_inc(s_q2, 1)
                    if some(s, j, 3):
                        moments(s, j, 3)
                    if some(s, j, -1):
                        residual(s, j, -1)
                    if some(s, j, 2):
                        q1_turned(s, j, 2)

                dve.memset(rnd[:], RND)
                stats(0, 0, 0)
                moments(0, 0, 0)
                for v in range(2):
                    for k in range(4):
                        first(v, 0, 0, k)
                    stats(v + 1, 0, 0)
                    moments(v + 1, 0, 0)
                    q1_turned(v, 0, 0)
                tiles(body)(dve)
                residual(NU - 1, 0, 0)

            @block.tensor
            def _(pe):
                def turn1(s, j, off):
                    pe.wait_ge(s_q1, num(s, j, off) + 1)
                    for c in range(C2):
                        last = pe.transpose(psM_b[:, c * P:(c + 1) * P], q1[:, c * P:(c + 1) * P], idb[:])
                    last.then_inc(s_q1p, 1)

                def gate_up(s, j, off):
                    v = num(s, j, off)
                    pe.wait_ge(s_q1t, v + 1)
                    for hf in range(2):
                        if not static(j) or s + off > 0:
                            pe.wait_ge(s_hm, 2 * v + hf - 1)
                        for w in range(2):
                            for c in range(C2):
                                last = pe.matmul(psT[:, hf, w], q1t[:, (s + off) % 2, c * P:(c + 1) * P], fwt[:, w, c * INNER + hf * 512:c * INNER + hf * 512 + 512],
                                                 start=(c == 0), stop=(c == C2 - 1))
                        last.then_inc(s_gu, 1)

                def turn2(s, j, off):
                    v = num(s, j, off)
                    pe.wait_ge(s_q2, v + 1)
                    if not static(j) or s + off > 0:
                        pe.wait_ge(s_q2t, v)
                    for c in range(NI):
                        last = pe.transpose(psU_b[:, c * P:(c + 1) * P], q2[:, (s + off) % 2, c * P:(c + 1) * P], idb[:])
                    last.then_inc(s_q2p, 1)

                def down(s, j, off):
                    v = num(s, j, off)
                    pe.wait_ge(s_q2t, v + 1)
                    if not static(j) or s + off > 1:
                        pe.wait_ge(s_res, num(s, j, off - 1))
                    for c in range(NI):
                        last = pe.matmul(psS[:, (s + off) % 2, 0:D], q2t[:, c * P:(c + 1) * P], fwt[:, 2, c * D:(c + 1) * D], start=(c == 0), stop=(c == NI - 1))
                    last.then_inc(s_dn, 1)

                def body(s, j):
                    if some(s, j, -1):
                        turn2(s, j, -1)
                    if some(s, j, 1):
                        gate_up(s, j, 1)
                    if some(s, j, -1):
                        down(s, j, -1)
                    if some(s, j, 2):
                        turn1(s, j, 2)

                turn1(0, 0, 0)
                gate_up(0, 0, 0)
                turn1(1, 0, 0)
                tiles(body)(pe)
                turn2(NU - 1, 0, 0)
                down(NU - 1, 0, 0)


_OUTS = [((B, S, D), "float32")]


def lay_out(v):
    v = {k: np.asarray(x) for k, x in v.items()}
    cols = np.array([[(2 * (2 * hq + g) + par) * HD + d for par in range(2) for d in range(HD) for hq in range(4)] for g in range(C2)]).ravel()

    def chunks(w):
        return w.reshape(-1, P, w.shape[-1]).transpose(1, 0, 2)

    def attn(q, k, vw, o):
        return np.stack([chunks(v[q].T[:, cols]), chunks(v[k].T[:, cols]), chunks(v[vw].T), chunks(v[o].T)], 1).reshape(P, -1)

    moe = np.stack([np.stack([chunks(v["L0_ffn_w1"][e].T).reshape(P, -1), chunks(v["L0_ffn_w3"][e].T).reshape(P, -1),
                              chunks(v["L0_ffn_w2"][e].T).reshape(P, -1)]) for e in range(E)]).reshape(3 * E, P, 2048)
    return {
        "x": v["x"].reshape(TOK, D),
        "ctx": v["ctx_1024"].transpose(0, 2, 1).reshape(B, C2, P, S).transpose(0, 2, 1, 3),
        "g": np.broadcast_to(np.stack([v["g_xattn"], v["g_ffn"]], 1).reshape(1, 4), (P, 4)),
        "gate": chunks(v["L0_ffn_gate_w"].T),
        "mask": chunks(v["mask_SxS2_ff0"]),
        "kpm": v["mask_BxS2_bf0"].view(np.int32),
        "bqk": np.stack([v[b][cols].reshape(C2, P).T for b in ("L1_xattn_b_q", "L1_xattn_b_k")], 1),
        "bv": np.broadcast_to(v["L1_xattn_b_v"], (P, D)),
        "bo": np.broadcast_to(v["L1_xattn_b_o"], (P, D)),
        "aw": np.stack([attn("L0_xattn_Wq", "L0_xattn_Wk", "L0_xattn_Wv", "L0_xattn_Wo"),
                        attn("L1_xattn_w_q", "L1_xattn_w_k", "L1_xattn_w_v", "L1_xattn_w_o")]),
        "moe": moe,
        "fw": np.stack([chunks(v["L1_ffn_w_gate"].T).reshape(P, -1), chunks(v["L1_ffn_w_up"].T).reshape(P, -1),
                        chunks(v["L1_ffn_w_down"].T).reshape(P, -1)]),
    }


def kernel(**inputs):
    import concourse.bacc as bacc
    from concourse.bass_utils import run_bass_kernel_spmd

    nc = bacc.Bacc("TRN2", target_bir_lowering=False, num_devices=1)
    arrays, aps = {}, {}
    for name, x in lay_out(inputs).items():
        arrays[f"in_{name}"] = np.ascontiguousarray(x)
        aps[name] = nc.dram_tensor(f"in_{name}", x.shape, mybir.dt.from_np(x.dtype), kind="ExternalInput").ap()
    out = nc.dram_tensor("out_0", (TOK, D), F32, kind="ExternalOutput").ap()
    build(nc, aps, out)
    r = run_bass_kernel_spmd(nc, [arrays], core_ids=[0])
    return r.results[0]["out_0"].reshape(B, S, D)
```
